# Optimizing a Trainium2 kernel written in Bass

```python
import numpy as np
import jax
import jax.numpy as jnp

def _softmax(x, axis=-1):
    return jax.nn.softmax(x, axis=axis)

def _gelu(x):
    return jax.nn.gelu(x, approximate=True)

def _silu(x):
    return jax.nn.silu(x)

def _sigmoid(x):
    return jax.nn.sigmoid(x)

def _layernorm(x, axis=-1, eps=1e-05):
    m = jnp.mean(x, axis=axis, keepdims=True)
    v = jnp.var(x, axis=axis, keepdims=True)
    return (x - m) / jnp.sqrt(v + eps)

def _scatter_add(tgt, idx, src, axis=0):
    return tgt.at[idx].add(src)

def _segment_sum(src, seg, n):
    return jax.ops.segment_sum(src, seg, n)
kernel_name = 'mk_adaln_d1_jaxref_r8_da27e5'

def setup_inputs(seed: int=0):
    np.random.seed(seed)
    _w = jnp.asarray

    def _L0_attn_setup():
        import jax, jax.numpy as jnp
        import numpy as np
        BATCH, L, D, N, K = (2, 256, 128, 32, 4)

        def _forward(x, in_proj_w, in_proj_b, conv_w, conv_b, A_log, B_w, B_b, C_w, C_b, dt_w, dt_b, out_w, out_b, ln_g, ln_beta):
            batch, seqlen, d = x.shape
            residual = x
            xz = x @ in_proj_w.T + in_proj_b
            xc, z = (xz[..., :d], xz[..., d:])
            xt = jnp.swapaxes(xc, 1, 2)
            conv = jax.lax.conv_general_dilated(xt, conv_w, window_strides=(1,), padding=[(2, 2)], feature_group_count=d, dimension_numbers=('NCH', 'OIH', 'NCH'))
            conv = conv + conv_b[None, :, None]
            xs = jax.nn.silu(jnp.swapaxes(conv, 1, 2)[:, :seqlen])
            A = -jnp.exp(jnp.clip(A_log, -5.0, 2.0))
            Bm = xs @ B_w.T + B_b
            Cm = xs @ C_w.T + C_b
            dt = jnp.clip(jax.nn.softplus(xs @ dt_w.T + dt_b), 0.001, 0.2)

            def step(state, inp):
                x_t, dt_t, B_t, C_t = inp
                A_bar = jnp.exp(dt_t[:, :, None] * A[None])
                B_bar = dt_t[:, :, None] * B_t[:, None, :]
                state = jnp.clip(state * A_bar + B_bar * x_t[:, :, None], -10.0, 10.0)
                y = jnp.einsum('bn,bdn->bd', C_t, state)
                return (state, y)
            init = jnp.zeros((batch, d, A.shape[1]), xs.dtype)
            seq = (jnp.swapaxes(xs, 0, 1), jnp.swapaxes(dt, 0, 1), jnp.swapaxes(Bm, 0, 1), jnp.swapaxes(Cm, 0, 1))
            _, ys = jax.lax.scan(step, init, seq)
            y = jnp.swapaxes(ys, 0, 1) * jax.nn.silu(z)
            out = y @ out_w.T + out_b + residual
            mu = out.mean(-1, keepdims=True)
            var = out.var(-1, keepdims=True)
            return ln_g * (out - mu) * jax.lax.rsqrt(var + 1e-05) + ln_beta
        key = jax.random.key(seed)
        ks = jax.random.split(key, 16)

        def nrm(k, shape, std=0.02, mean=0.0):
            return mean + std * jax.random.normal(k, shape, jnp.float32)
        lim = 1.0 / np.sqrt(D)
        return {'x': jax.random.normal(ks[0], (BATCH, L, D), jnp.float32), 'in_proj_w': jax.random.uniform(ks[1], (2 * D, D), jnp.float32, -lim, lim), 'in_proj_b': jax.random.uniform(ks[2], (2 * D,), jnp.float32, -lim, lim), 'conv_w': jax.random.uniform(ks[3], (D, 1, K), jnp.float32, -0.5, 0.5), 'conv_b': jax.random.uniform(ks[4], (D,), jnp.float32, -0.5, 0.5), 'A_log': nrm(ks[5], (D, N), std=0.1, mean=-2.0), 'B_w': nrm(ks[6], (N, D)), 'B_b': jnp.zeros((N,), jnp.float32), 'C_w': nrm(ks[7], (N, D)), 'C_b': jnp.zeros((N,), jnp.float32), 'dt_w': nrm(ks[8], (D, D)), 'dt_b': jnp.zeros((D,), jnp.float32), 'out_w': nrm(ks[9], (D, D)), 'out_b': jnp.zeros((D,), jnp.float32), 'ln_g': jnp.ones((D,), jnp.float32), 'ln_beta': jnp.zeros((D,), jnp.float32)}
    _L0_attn_in = _L0_attn_setup()

    def _L0_ffn_setup():
        import jax, jax.numpy as jnp
        import numpy as np
        TOP_K = 2

        def _gelu(x):
            return jax.nn.gelu(x, approximate=False)
        key = jax.random.key(seed)
        ks = jax.random.split(key, 6)
        B, S, D, F, E = (2, 256, 128, 256, 8)
        sc_g = 1.0 / np.sqrt(D)

        def xav(k, shape, fan_in, fan_out):
            lim = np.sqrt(6.0 / (fan_in + fan_out))
            return jax.random.uniform(k, shape, jnp.float32, -lim, lim)
        return {'x': jax.random.normal(ks[0], (B, S, D), jnp.float32), 'Wg': xav(ks[1], (D, E), D, E), 'Wu': xav(ks[2], (E, D, F), D, F), 'Wd': xav(ks[3], (E, F, D), F, D), 'W1': xav(ks[4], (D, F), D, F), 'W2': xav(ks[5], (F, D), F, D)}
    _L0_ffn_in = _L0_ffn_setup()
    _L0_c = _w((lambda *s: np.random.randn(*s).astype(np.float32) * 0.05)(32, 128))
    _L0_wmod = _w((lambda *s: np.random.randn(*s).astype(np.float32) * 0.05)(128, 6 * 128) * 128 ** (-0.5))
    _d = {'L0_attn_x': _L0_attn_in['x'], 'L0_attn_in_proj_w': _L0_attn_in['in_proj_w'], 'L0_attn_in_proj_b': _L0_attn_in['in_proj_b'], 'L0_attn_conv_w': _L0_attn_in['conv_w'], 'L0_attn_conv_b': _L0_attn_in['conv_b'], 'L0_attn_A_log': _L0_attn_in['A_log'], 'L0_attn_B_w': _L0_attn_in['B_w'], 'L0_attn_B_b': _L0_attn_in['B_b'], 'L0_attn_C_w': _L0_attn_in['C_w'], 'L0_attn_C_b': _L0_attn_in['C_b'], 'L0_attn_dt_w': _L0_attn_in['dt_w'], 'L0_attn_dt_b': _L0_attn_in['dt_b'], 'L0_attn_out_w': _L0_attn_in['out_w'], 'L0_attn_out_b': _L0_attn_in['out_b'], 'L0_attn_ln_g': _L0_attn_in['ln_g'], 'L0_attn_ln_beta': _L0_attn_in['ln_beta'], 'L0_ffn_Wg': _L0_ffn_in['Wg'], 'L0_ffn_Wu': _L0_ffn_in['Wu'], 'L0_ffn_Wd': _L0_ffn_in['Wd'], 'L0_ffn_W1': _L0_ffn_in['W1'], 'L0_ffn_W2': _L0_ffn_in['W2'], 'L0_c': _L0_c, 'L0_wmod': _L0_wmod}
    _x0 = _d['L0_attn_x']
    _d['L0_attn_x'] = jax.random.normal(jax.random.fold_in(jax.random.key(seed), 1), (32, 256, 128), dtype=_x0.dtype)
    del _x0
    return _d

def reference(L0_attn_x, L0_attn_in_proj_w, L0_attn_in_proj_b, L0_attn_conv_w, L0_attn_conv_b, L0_attn_A_log, L0_attn_B_w, L0_attn_B_b, L0_attn_C_w, L0_attn_C_b, L0_attn_dt_w, L0_attn_dt_b, L0_attn_out_w, L0_attn_out_b, L0_attn_ln_g, L0_attn_ln_beta, L0_ffn_Wg, L0_ffn_Wu, L0_ffn_Wd, L0_ffn_W1, L0_ffn_W2, L0_c, L0_wmod):

    def _L0_attn_ref(x, in_proj_w, in_proj_b, conv_w, conv_b, A_log, B_w, B_b, C_w, C_b, dt_w, dt_b, out_w, out_b, ln_g, ln_beta):
        import jax, jax.numpy as jnp
        import numpy as np
        BATCH, L, D, N, K = (2, 256, 128, 32, 4)

        def _forward(x, in_proj_w, in_proj_b, conv_w, conv_b, A_log, B_w, B_b, C_w, C_b, dt_w, dt_b, out_w, out_b, ln_g, ln_beta):
            batch, seqlen, d = x.shape
            residual = x
            xz = x @ in_proj_w.T + in_proj_b
            xc, z = (xz[..., :d], xz[..., d:])
            xt = jnp.swapaxes(xc, 1, 2)
            conv = jax.lax.conv_general_dilated(xt, conv_w, window_strides=(1,), padding=[(2, 2)], feature_group_count=d, dimension_numbers=('NCH', 'OIH', 'NCH'))
            conv = conv + conv_b[None, :, None]
            xs = jax.nn.silu(jnp.swapaxes(conv, 1, 2)[:, :seqlen])
            A = -jnp.exp(jnp.clip(A_log, -5.0, 2.0))
            Bm = xs @ B_w.T + B_b
            Cm = xs @ C_w.T + C_b
            dt = jnp.clip(jax.nn.softplus(xs @ dt_w.T + dt_b), 0.001, 0.2)

            def step(state, inp):
                x_t, dt_t, B_t, C_t = inp
                A_bar = jnp.exp(dt_t[:, :, None] * A[None])
                B_bar = dt_t[:, :, None] * B_t[:, None, :]
                state = jnp.clip(state * A_bar + B_bar * x_t[:, :, None], -10.0, 10.0)
                y = jnp.einsum('bn,bdn->bd', C_t, state)
                return (state, y)
            init = jnp.zeros((batch, d, A.shape[1]), xs.dtype)
            seq = (jnp.swapaxes(xs, 0, 1), jnp.swapaxes(dt, 0, 1), jnp.swapaxes(Bm, 0, 1), jnp.swapaxes(Cm, 0, 1))
            _, ys = jax.lax.scan(step, init, seq)
            y = jnp.swapaxes(ys, 0, 1) * jax.nn.silu(z)
            out = y @ out_w.T + out_b + residual
            mu = out.mean(-1, keepdims=True)
            var = out.var(-1, keepdims=True)
            return ln_g * (out - mu) * jax.lax.rsqrt(var + 1e-05) + ln_beta
        return _forward(x, in_proj_w, in_proj_b, conv_w, conv_b, A_log, B_w, B_b, C_w, C_b, dt_w, dt_b, out_w, out_b, ln_g, ln_beta)

    def _L0_ffn_ref(x, Wg, Wu, Wd, W1, W2):
        import jax, jax.numpy as jnp
        import numpy as np
        TOP_K = 2

        def _gelu(x):
            return jax.nn.gelu(x, approximate=False)
        B, S, D = x.shape
        E = Wu.shape[0]
        T = B * S
        xt = x.reshape(T, D)
        probs = jax.nn.softmax(xt @ Wg, axis=-1)
        topv, topi = jax.lax.top_k(probs, TOP_K)
        topv = topv / jnp.sum(topv, axis=-1, keepdims=True)
        cw = jnp.zeros((T, E), x.dtype).at[jnp.arange(T)[:, None], topi].set(topv)
        h = _gelu(jnp.einsum('td,edf->tef', xt, Wu))
        y = jnp.einsum('tef,efd->ted', h, Wd)
        moe = jnp.einsum('ted,te->td', y, cw)
        shared = _gelu(xt @ W1) @ W2
        return (shared + moe).reshape(B, S, D)
    x = L0_attn_x
    mod = (_silu(L0_c) @ L0_wmod).reshape(L0_c.shape[0], 6, 1, -1)
    sa, ca, ga, sb, cb, gb = (mod[:, 0], mod[:, 1], mod[:, 2], mod[:, 3], mod[:, 4], mod[:, 5])
    ga = (2 * (ga >= 0) - 1) * jnp.maximum(jnp.abs(ga), 0.25)
    gb = (2 * (gb >= 0) - 1) * jnp.maximum(jnp.abs(gb), 0.25)
    h = _layernorm(x, axis=-1) * (1 + ca) + sa
    x = x + ga * _L0_attn_ref(h, L0_attn_in_proj_w, L0_attn_in_proj_b, L0_attn_conv_w, L0_attn_conv_b, L0_attn_A_log, L0_attn_B_w, L0_attn_B_b, L0_attn_C_w, L0_attn_C_b, L0_attn_dt_w, L0_attn_dt_b, L0_attn_out_w, L0_attn_out_b, L0_attn_ln_g, L0_attn_ln_beta)
    h = _layernorm(x, axis=-1) * (1 + cb) + sb
    x = x + gb * _L0_ffn_ref(h, L0_ffn_Wg, L0_ffn_Wu, L0_ffn_Wd, L0_ffn_W1, L0_ffn_W2)
    return x

_drawn_inputs = setup_inputs


def setup_inputs(seed=0):
    import zlib

    import numpy as np

    out = dict(_drawn_inputs(seed))
    spreads = {'L0_attn_B_b': (0.0, 0.8),
     'L0_attn_C_b': (0.0, 2.0),
     'L0_attn_dt_b': (0.0, 0.792),
     'L0_attn_out_b': (0.0, 2.0),
     'L0_attn_ln_g': (1.0, 0.2),
     'L0_attn_ln_beta': (0.0, 0.278)}
    factors = {'L0_attn_in_proj_w': 8.0,
     'L0_attn_in_proj_b': 8.0,
     'L0_attn_conv_w': 8.0,
     'L0_attn_conv_b': 8.0,
     'L0_attn_A_log': 8.0,
     'L0_attn_B_w': 8.0,
     'L0_attn_C_w': 8.0,
     'L0_attn_out_w': 8.0}
    for name, (base, spread) in spreads.items():
        noise = np.random.default_rng([zlib.crc32(name.encode()), seed]).standard_normal(out[name].shape)
        drawn = base * np.exp(spread * noise) if base else spread * noise
        out[name] = jnp.asarray(drawn.astype(out[name].dtype))
    for name, factor in factors.items():
        out[name] = (out[name] * factor).astype(out[name].dtype)
    return out
```

```python
from contextlib import ExitStack

import numpy as np

import concourse.bass as bass
from concourse import mybir

F32 = mybir.dt.float32
U32 = mybir.dt.uint32
ALU = mybir.AluOpType
ACT = mybir.ActivationFunctionType

NB, L, D, N, K = 32, 256, 128, 32, 4
F, E, MOD = 256, 8, 6
P = 128
T = 16
TOK = T * NB
NT = TOK // P
SPT = P // NB
CH = L // T
BQ = P // N
BG = NB // BQ
HT = T // 2
FT = F // P
EX = E + 1
HBUF = 3
CLIP, EPS = 10.0, 1e-5
DT_MIN, DT_MAX, DT_IN_MAX = 0.001, 0.2, 20.0
GATE_MIN = 0.25

UP_AT = (0, 0, 1, 5, 5, 6, 10, 10, 11)
DOWN_AT = (1, 2, 3, 6, 7, 8, 11, 12, 13)

WORK = [
    (0, "a", "scan", "dtx1"), (0, "c", "scan", "c1"),
    (1, "a", "post", "proj"), (1, "c", "ffn", "down0"),
    (2, "a", "prep", "turn"), (2, "b", "prep", "turn_next"), (2, "c", "ffn", "down1"),
    (3, "a", "prep", "xc"), (3, "c", "ffn", "down2"),
    (4, "a", "prep", "xc_next"),
    (6, "c", "ffn", "down3"),
    (7, "a", "prep", "z"), (7, "c", "ffn", "down4"),
    (8, "a", "prep", "dt"), (8, "b", "prep", "b"), (8, "c", "ffn", "down5"),
    (9, "a", "prep", "c0"),
    (10, "a", "prep", "dtx0"),
    (11, "c", "ffn", "down6"), (12, "c", "ffn", "down7"), (13, "c", "ffn", "down8"),
    (15, "a", "post", "turn2"), (15, "c", "post", "logits"),
]
STAGES = ("prep", "scan", "post", "ffn")
LAG = {"prep": -1, "scan": 0, "post": 1, "ffn": 2}
USES = {s: sum(u[2] == s for u in WORK) for s in STAGES}
FULL_FROM, FULL_TO = 2, CH - 2
LOOP_FROM, LOOP_TO = FULL_FROM + 1, CH - 1


def active(stage, c):
    return not isinstance(c, int) or 0 <= c - LAG[stage] < CH


def work_before(c):
    if isinstance(c, int):
        return sum(USES[s] * min(max(c - LAG[s], 0), CH) for s in STAGES)
    return c * sum(USES.values()) - sum(USES[s] * LAG[s] for s in STAGES)


def work_count(name, c):
    n = 0
    for _, _, stage, use in WORK:
        n += active(stage, c)
        if use == name:
            return work_before(c) + n
    raise KeyError(name)


def macros(eng, body, loop_to=LOOP_TO):
    for c in range(-1, LOOP_FROM):
        body(c)
    with eng.Fori(LOOP_FROM, loop_to) as c:
        body(c)
    for c in range(loop_to, CH + 2):
        body(c)


def adaln_block(nc, x, in_w, in_b, conv_w, conv_b, a_log, b_w, b_b, c_w, c_b, dt_w, dt_b, out_w, out_b,
                ln_g, ln_beta, wg, wu, wd, c_t, wmod, out):
    ctx = ExitStack()
    with ctx:
        def sb(name, shape, dt=F32):
            return ctx.enter_context(nc.sbuf_tensor(name, shape, dt))

        def ps(name, shape):
            return ctx.enter_context(nc.psum_tensor(name, shape, F32))

        def sem(name):
            return ctx.enter_context(nc.semaphore(name))

        in_w_sb = sb("in_w_sb", [P, 2 * D])
        dt_w_sb = sb("dt_w_sb", [P, D])
        b_w_sb = sb("b_w_sb", [P, N])
        c_w_sb = sb("c_w_sb", [P, BQ * N])
        out_w_sb = sb("out_w_sb", [P, D])
        wg_sb = sb("wg_sb", [P, E])
        wu_sb = sb("wu_sb", [P, EX, F])
        wd_sb = sb("wd_sb", [P, EX, FT, D])
        wmod_sb = sb("wmod_sb", [P, MOD * D])
        cond = sb("cond", [P, P])
        in_b_sb = sb("in_b_sb", [P, 2])
        conv_w_sb = sb("conv_w_sb", [P, K])
        conv_b_sb = sb("conv_b_sb", [P, 1])
        neg_a = sb("neg_a", [P, N])
        b_b_row = sb("b_b_row", [P, 1, N])
        c_b_col = sb("c_b_col", [P, 1])
        dt_b_sb = sb("dt_b_sb", [P, 1])
        out_b_row = sb("out_b_row", [P, 1, D])
        g_row = sb("g_row", [P, D])
        beta_row = sb("beta_row", [P, D])
        ident = sb("ident", [P, P])
        shift_a = sb("shift_a", [P, 1, D])
        scale_a = sb("scale_a", [P, 1, D])
        gate_g = sb("gate_g", [P, 1, D])
        gate_beta = sb("gate_beta", [P, 1, D])
        shift_b = sb("shift_b", [P, 1, D])
        scale_b = sb("scale_b", [P, 1, D])
        gate_b = sb("gate_b", [P, 1, D])
        gate_t = sb("gate_t", [P, 4, D])
        batch_mask = sb("batch_mask", [P, NB])
        group_mask = sb("group_mask", [P, BQ])
        edge = sb("edge", [P, CH])
        eps_t = sb("eps_t", [P, 1])
        minus_half = sb("minus_half", [P, 1])
        zero_t = sb("zero_t", [P, 1])
        iota_e = sb("iota_e", [P, 1, E])

        x_in = sb("x_in", [P, NT + 1, D])
        bn1 = sb("bn1", [P, NT + 1, 6])
        mv1 = sb("mv1", [P, NT + 1, 2])
        ve1 = sb("ve1", [P, NT + 1])
        rstd1 = sb("rstd1", [P, NT + 1])
        xn = sb("xn", [P, NT + 1, D])
        h = sb("h", [P, NT + 1, D])
        h_res = sb("h_res", [P, 2, TOK])
        h_t = sb("h_t", [P, TOK + NB])
        xc = sb("xc", [P, (T + K - 1) * NB])
        cv = sb("cv", [P, TOK])
        cv_tap = sb("cv_tap", [P, TOK])
        xs = sb("xs", [P, TOK])
        z_act = sb("z_act", [P, 2, TOK])
        dt_raw = sb("dt_raw", [P, TOK])
        dt_exp = sb("dt_exp", [P, TOK])
        dt = sb("dt", [P, TOK])
        dtx = sb("dtx", [P, TOK])
        dtx_tok = sb("dtx_tok", [P, NT, D])
        b_tok = sb("b_tok", [P, NT, N])
        b_diag = sb("b_diag", [P, 2, NB, N])
        c_diag = sb("c_diag", [P, TOK])
        decay = sb("decay", [P, T, NB, N])
        state = sb("state", [P, 2, BG * D])
        prod = sb("prod", [P, BG * D])
        total = sb("total", [P, BG * D])
        yz = sb("yz", [P, TOK])
        o = sb("o", [P, NT, D])
        bn2 = sb("bn2", [P, NT, 6])
        mv2 = sb("mv2", [P, NT, 2])
        ve2 = sb("ve2", [P, NT])
        rstd2 = sb("rstd2", [P, NT])
        x_res = sb("x_res", [P, NT, D])
        x2 = sb("x2", [P, NT, D])
        bn3 = sb("bn3", [P, NT, 6])
        mv3 = sb("mv3", [P, NT, 2])
        ve3 = sb("ve3", [P, NT])
        rstd3 = sb("rstd3", [P, NT])
        h2 = sb("h2", [P, NT, D])
        h2_t = sb("h2_t", [P, TOK])
        lg = sb("lg", [P, NT, E])
        top_v = sb("top_v", [P, NT, 8])
        top_i = sb("top_i", [P, NT, 8], U32)
        top_f = sb("top_f", [P, NT, 2])
        rt = sb("rt", [P, 4, NT])
        pick = sb("pick", [P, 2, NT, E])
        cw = sb("cw", [P, NT, E])
        hid = sb("hid", [P, HBUF, FT, TOK])
        scaled = sb("scaled", [P, 2, TOK])
        acc = sb("acc", [P, NT, D])
        x2_keep = sb("x2_keep", [P, NT, D])
        out_sb = sb("out_sb", [P, NT, D])

        decay_ps = ps("decay_ps", [P, BG, D])
        input_ps = ps("input_ps", [P, BG, D])
        y_ps = ps("y_ps", [P, TOK])
        up_ps = [ps(f"up_ps{f}", [P, TOK]) for f in range(FT)]
        work = ps("work", [P, TOK])

        params_in = sem("params_in")
        ffn_in = sem("ffn_in")
        ident_set = sem("ident_set")
        diag_set = sem("diag_set")
        consts_set = sem("consts_set")
        cond_ready = sem("cond_ready")
        mod_ready = sem("mod_ready")
        set_up = sem("set_up")
        a_exp = sem("a_exp")
        started = sem("started")
        work_full = sem("work_full")
        work_read = sem("work_read")
        x_loaded = sem("x_loaded")
        mv1_done = sem("mv1_done")
        ve1_done = sem("ve1_done")
        rstd1_done = sem("rstd1_done")
        xn_done = sem("xn_done")
        h_scaled = sem("h_scaled")
        h_done = sem("h_done")
        h_res_done = sem("h_res_done")
        conv_step = sem("conv_step")
        xs_done = sem("xs_done")
        dt_exp_done = sem("dt_exp_done")
        dt_log_done = sem("dt_log_done")
        dt_done = sem("dt_done")
        dtx_done = sem("dtx_done")
        b_diag_done = sem("b_diag_done")
        decay_made = [sem("decay_made0"), sem("decay_made1")]
        decay_turned = sem("decay_turned")
        input_made = sem("input_made")
        decayed = sem("decayed")
        added = sem("added")
        state_done = sem("state_done")
        y_done = sem("y_done")
        yz_done = sem("yz_done")
        x_res_loaded = sem("x_res_loaded")
        mv2_done = sem("mv2_done")
        ve2_done = sem("ve2_done")
        rstd2_done = sem("rstd2_done")
        on_done = sem("on_done")
        x2_step = sem("x2_step")
        mv3_done = sem("mv3_done")
        ve3_done = sem("ve3_done")
        rstd3_done = sem("rstd3_done")
        n2_done = sem("n2_done")
        h2_step = sem("h2_step")
        index_done = sem("index_done")
        gap_done = sem("gap_done")
        gap_exp = sem("gap_exp")
        route_step = sem("route_step")
        up_done = [sem(f"up_done{f}") for f in range(FT)]
        gelu_done = [sem(f"gelu_done{f}") for f in range(FT)]
        acc_step = sem("acc_step")
        kept = sem("kept")
        final_step = sem("final_step")
        stored = sem("stored")

        block = ctx.enter_context(nc.Block())

        params = [(in_w_sb[:, :], in_w), (in_b_sb[:, :], in_b), (conv_w_sb[:, :], conv_w), (conv_b_sb[:, :], conv_b),
                  (neg_a[:, :], a_log), (b_w_sb[:, :], b_w), (b_b_row[:, 0, :], b_b), (c_w_sb[:, :], c_w),
                  (c_b_col[:, :], c_b), (dt_w_sb[:, :], dt_w), (dt_b_sb[:, :], dt_b), (out_w_sb[:, :], out_w),
                  (out_b_row[:, 0, :], out_b), (g_row[:, :], ln_g), (beta_row[:, :], ln_beta), (wg_sb[:, :], wg),
                  (cond[:, :], c_t), (wmod_sb[:, :], wmod)]
        x_steps = x.rearrange("b (c j t) d -> c t b j d", c=CH, t=SPT)
        out_steps = out.rearrange("b (c j t) d -> c t b j d", c=CH, t=SPT)
        LOADS = 16 * (SPT + 1)
        MOVES = 16 * SPT

        def rows(t):
            return slice(t * NB, (t + 1) * NB)

        def at_step(k):
            return [u[1:] for u in WORK if u[0] == k]

        @block.sync
        def _(sp):
            def load_x(q):
                for t in range(SPT):
                    sp.dma_start(x_in[rows(t), 0:NT, :], x_steps[q, t]).then_inc(x_loaded, 16)
                ahead = min(q + 1, CH - 1) if isinstance(q, int) else q + 1
                sp.dma_start(x_in[rows(0), NT, :], x_steps[ahead, 0][:, 0, :]).then_inc(x_loaded, 16)

            for i, (dst, src) in enumerate(params):
                if i % 2 == 0:
                    sp.dma_start(dst, src).then_inc(params_in, 16)
            sp.wait_ge(set_up, 1)
            load_x(0)
            sp.dma_start(wu_sb[:, :, :], wu).then_inc(ffn_in, 16)
            sp.dma_start(wd_sb[:, :, :, :], wd).then_inc(ffn_in, 16)

            def body(c):
                if active("prep", c) and (not isinstance(c, int) or c + 2 < CH):
                    sp.wait_ge(xn_done, (NT + 1) * (c + 2))
                    load_x(c + 2)
                if active("scan", c):
                    if not isinstance(c, int) or c >= 1:
                        sp.wait_ge(x2_step, 3 * c)
                    for t in range(SPT):
                        sp.dma_start(x_res[rows(t), :, :], x_steps[c, t]).then_inc(x_res_loaded, 16)
                if active("ffn", c):
                    sp.wait_ge(final_step, 2 * (c - 1))
                    for t in range(SPT):
                        sp.dma_start(out_steps[c - 2, t], out_sb[rows(t), :, :]).then_inc(stored, 16)

            macros(sp, body, loop_to=CH - 3)
            sp.wait_ge(stored, MOVES * CH)

        @block.gpsimd
        def _(pool):
            nc.gpsimd.memset(ident[:, :], 0.0).then_inc(ident_set, 1)
            nc.gpsimd.memset(batch_mask[:, :], 0.0).then_inc(ident_set, 1)
            pool.wait_ge(ident_set, 2)
            nc.gpsimd.affine_select(out=ident[:, :], in_=ident[:, :], compare_op=ALU.not_equal, fill=1.0, base=0,
                                    pattern=[[-1, P]], channel_multiplier=1).then_inc(diag_set, 1)
            for t in range(SPT):
                pool.wait_ge(diag_set, t + 1)
                nc.gpsimd.affine_select(out=batch_mask[:, :], in_=batch_mask[:, :], compare_op=ALU.not_equal, fill=1.0,
                                        base=-t * NB, pattern=[[-1, NB]], channel_multiplier=1).then_inc(diag_set, 1)
            pool.wait_ge(diag_set, SPT + 1)
            pool.wait_ge(started, 1)

            def settle():
                pool.wait_ge(started, 1)

            def inverse_root(var, ve, rstd, n, mv_done, ve_done, rstd_done, q, per):
                pool.wait_ge(mv_done, per * (q + 1))
                nc.gpsimd.tensor_tensor(ve[:, :], var, eps_t[:, 0:1].broadcast_to([P, n]), ALU.add).then_inc(ve_done, 1)
                pool.wait_ge(ve_done, q + 1)
                nc.gpsimd.tensor_tensor(rstd[:, :], ve[:, :], minus_half[:, 0:1].broadcast_to([P, n]),
                                        ALU.pow).then_inc(rstd_done, 1)

            def make_b_diag(j, q):
                if j >= 2:
                    pool.wait_ge(input_made, T * q + SPT * (j - 1))
                elif not isinstance(q, int) or q >= 1:
                    pool.wait_ge(input_made, T * q - SPT * (1 - j))
                if j == 0:
                    pool.wait_ge(work_read, work_count("b", q - 1))
                nc.gpsimd.tensor_tensor(
                    b_diag[:, j % 2, :, :], b_tok[:, j:j + 1, :].broadcast_to([P, NB, N]),
                    batch_mask[:, :].unsqueeze(2).broadcast_to([P, NB, N]), ALU.mult).then_inc(b_diag_done, 1)

            def body(c):
                prep, scan, post, ffn = (active(s, c) for s in STAGES)
                later = not isinstance(c, int)
                for k in range(T):
                    if k == 0 and ffn:
                        q = c - 2
                        pool.wait_ge(x2_step, 3 * (q + 1))
                        if later or q >= 1:
                            pool.wait_ge(final_step, 2 * q)
                        nc.gpsimd.tensor_tensor(x2_keep[:, :, :], x2[:, :, :],
                                                zero_t[:, 0:1].unsqueeze(2).broadcast_to([P, NT, D]), ALU.add).then_inc(kept, 1)
                    if k == 1 and prep:
                        q = c + 1
                        inverse_root(mv1[:, :, 1], ve1, rstd1, NT + 1, mv1_done, ve1_done, rstd1_done, q, NT + 1)
                        pool.wait_ge(xn_done, (NT + 1) * (q + 1))
                        if later or q >= 1:
                            pool.wait_ge(work_full, work_count("turn_next", c - 1))
                            pool.wait_ge(h_res_done, q)
                        nc.gpsimd.tensor_tensor(h[:, :, :], xn[:, :, :], scale_a[:, :, :].broadcast_to([P, NT + 1, D]),
                                                ALU.mult).then_inc(h_scaled, 1)
                        pool.wait_ge(h_scaled, q + 1)
                        nc.gpsimd.tensor_tensor(h[:, :, :], h[:, :, :], shift_a[:, :, :].broadcast_to([P, NT + 1, D]),
                                                ALU.add).then_inc(h_done, 1)
                    if k == 2 and post:
                        q = c - 1
                        inverse_root(mv2[:, :, 1], ve2, rstd2, NT, mv2_done, ve2_done, rstd2_done, q, NT)
                    if k == 3:
                        if scan:
                            make_b_diag(2, c)
                        if post:
                            q = c - 1
                            pool.wait_ge(on_done, NT * (q + 1))
                            nc.gpsimd.tensor_tensor(o[:, :, :], o[:, :, :], gate_g[:, :, :].broadcast_to([P, NT, D]),
                                                    ALU.mult).then_inc(x2_step, 1)
                            pool.wait_ge(x2_step, 3 * q + 1)
                            nc.gpsimd.tensor_tensor(o[:, :, :], o[:, :, :], gate_beta[:, :, :].broadcast_to([P, NT, D]),
                                                    ALU.add).then_inc(x2_step, 1)
                            pool.wait_ge(x2_step, 3 * q + 2)
                            pool.wait_ge(x_res_loaded, MOVES * (q + 1))
                            if later or q >= 1:
                                pool.wait_ge(kept, q)
                                pool.wait_ge(n2_done, NT * q)
                            nc.gpsimd.tensor_tensor(x2[:, :, :], o[:, :, :], x_res[:, :, :], ALU.add).then_inc(x2_step, 1)
                    if k == 4 and prep:
                        q = c + 1
                        pool.wait_ge(work_read, work_count("xc_next", c))
                        if later or q >= 1:
                            pool.wait_ge(xs_done, q)
                        n = (K + K) * q
                        for tap in range(K):
                            dst = cv if tap == 0 else cv_tap
                            if tap >= 2:
                                n_ = (n + 2 * tap - 1)
                                pool.wait_ge(conv_step, n_)
                            nc.gpsimd.tensor_tensor(dst[:, :], xc[:, tap * NB:tap * NB + TOK],
                                                    conv_w_sb[:, tap:tap + 1].broadcast_to([P, TOK]), ALU.mult)\
                              .then_inc(conv_step, 1)
                            if tap >= 1:
                                pool.wait_ge(conv_step, n + 2 * tap)
                                nc.gpsimd.tensor_tensor(cv[:, :], cv[:, :], cv_tap[:, :], ALU.add).then_inc(conv_step, 1)
                        pool.wait_ge(conv_step, n + 2 * K - 1)
                        nc.gpsimd.tensor_tensor(xc[:, 0:2 * NB], xc[:, TOK:TOK + 2 * NB],
                                                zero_t[:, 0:1].broadcast_to([P, 2 * NB]), ALU.add).then_inc(conv_step, 1)
                    if k == 5 and post:
                        q = c - 1
                        inverse_root(mv3[:, :, 1], ve3, rstd3, NT, mv3_done, ve3_done, rstd3_done, q, NT)
                    if k == 6 and prep:
                        q = c + 1
                        if later or q >= 2:
                            pool.wait_ge(work_read, work_count("proj", c))
                        settle()
                        nc.gpsimd.tensor_tensor(h_res[:, q % 2, :].rearrange("p (j d) -> p j d", j=NT), h[:, 0:NT, :],
                                                out_b_row[:, :, :].broadcast_to([P, NT, D]), ALU.add).then_inc(h_res_done, 1)
                    if k == 7:
                        if scan:
                            make_b_diag(3, c)
                        if post:
                            q = c - 1
                            pool.wait_ge(n2_done, NT * (q + 1))
                            nc.gpsimd.tensor_tensor(h2[:, :, :], h2[:, :, :], scale_b[:, :, :].broadcast_to([P, NT, D]),
                                                    ALU.mult).then_inc(h2_step, 1)
                            pool.wait_ge(h2_step, 2 * q + 1)
                            nc.gpsimd.tensor_tensor(h2[:, :, :], h2[:, :, :], shift_b[:, :, :].broadcast_to([P, NT, D]),
                                                    ALU.add).then_inc(h2_step, 1)
                    if k == 9 and prep:
                        q = c + 1
                        pool.wait_ge(dt_done, q + 1)
                        if later or q >= 1:
                            pool.wait_ge(work_full, work_count("dtx1", c))
                        nc.gpsimd.tensor_tensor(dtx[:, :], dt[:, :], xs[:, :], ALU.mult).then_inc(dtx_done, 1)
                    if k == 12 and prep:
                        make_b_diag(0, c + 1)
                    if k == 15 and prep:
                        make_b_diag(1, c + 1)
                    for e in range(1, EX):
                        if ffn and DOWN_AT[e] == k:
                            q = c - 2
                            pool.wait_ge(work_read, work_count(f"down{e}", c))
                            if e >= 2:
                                pool.wait_ge(acc_step, E * q + e - 1)
                            nc.gpsimd.tensor_tensor(acc[:, :, :], acc[:, :, :],
                                                    scaled[:, e % 2, :].rearrange("p (j d) -> p j d", j=NT),
                                                    ALU.add).then_inc(acc_step, 1)
                    if k == 14 and ffn:
                        q = c - 2
                        pool.wait_ge(acc_step, E * (q + 1))
                        if later or q >= 1:
                            pool.wait_ge(stored, MOVES * q)
                        nc.gpsimd.tensor_tensor(out_sb[:, :, :], acc[:, :, :], gate_b[:, :, :].broadcast_to([P, NT, D]),
                                                ALU.mult).then_inc(final_step, 1)
                        pool.wait_ge(final_step, 2 * q + 1)
                        pool.wait_ge(kept, q + 1)
                        nc.gpsimd.tensor_tensor(out_sb[:, :, :], out_sb[:, :, :], x2_keep[:, :, :],
                                                ALU.add).then_inc(final_step, 1)

            macros(pool, body)

        @block.scalar
        def _(act):
            for i, (dst, src) in enumerate(params):
                if i % 2 == 1:
                    act.dma_start(dst, src).then_inc(params_in, 16)
            act.wait_ge(params_in, 16 * len(params))
            nc.scalar.activation(cond[:, :], cond[:, :], ACT.Silu).then_inc(cond_ready, 1)
            act.wait_ge(set_up, 2)
            nc.scalar.activation(neg_a[:, :], neg_a[:, :], ACT.Exp).then_inc(a_exp, 1)
            act.wait_ge(started, 1)

            def settle():
                act.wait_ge(started, 1)

            def full(name, c):
                act.wait_ge(work_full, work_count(name, c))

            def decays(half, q, n0, n1):
                if n0 == 0:
                    act.wait_ge(dt_done, q + 1)
                    if not isinstance(q, int) or q >= 1:
                        act.wait_ge(decay_turned, T * (q - 1) + HT * (half + 1))
                for n in range(n0, n1):
                    nc.scalar.activation(decay[:, half * HT:(half + 1) * HT, :, n],
                                         dt[:, half * HT * NB:(half + 1) * HT * NB].rearrange("p (t b) -> p t b", b=NB),
                                         ACT.Exp, scale=neg_a[:, n:n + 1]).then_inc(decay_made[half], 1)

            def gelu(e, q):
                for f in range(FT):
                    act.wait_ge(up_done[f], EX * q + e + 1)
                    if f == 0 and (e >= HBUF or not isinstance(q, int) or q >= 1):
                        old = (e - HBUF, q) if e >= HBUF else (e - HBUF + EX, q - 1)
                        act.wait_ge(work_full, work_count(f"down{old[0]}", old[1] + 2))
                    nc.scalar.activation(hid[:, e % HBUF, f, :], up_ps[f][:, :], ACT.Gelu).then_inc(gelu_done[f], 1)

            def body(c):
                prep, scan, post, ffn = (active(s, c) for s in STAGES)
                later = not isinstance(c, int)
                for k in range(T):
                    if ffn:
                        for e in range(EX):
                            if UP_AT[e] == k:
                                gelu(e, c - 2)
                    if k == 0 and scan:
                        full("dtx1", c)
                        if later or c >= 1:
                            act.wait_ge(input_made, T * c)
                        nc.scalar.activation(dtx_tok[:, NT // 2:NT, :],
                                             work[:, 0:TOK // 2].rearrange("p (j d) -> p j d", d=D),
                                             ACT.Copy).then_inc(work_read, 1)
                    if k == 2:
                        if prep:
                            full("turn", c)
                            nc.scalar.activation(h_t[:, 0:TOK], work[:, :], ACT.Copy).then_inc(work_read, 1)
                            full("turn_next", c)
                            nc.scalar.activation(h_t[:, TOK:], work[:, 0:NB], ACT.Copy).then_inc(work_read, 1)
                        if scan:
                            decays(1, c, 0, 11)
                    if k == 3:
                        if prep:
                            full("xc", c)
                            if later or c >= 0:
                                act.wait_ge(conv_step, 2 * K * (c + 1))
                            nc.scalar.activation(xc[:, 2 * NB:2 * NB + TOK], work[:, :], ACT.Identity,
                                                 bias=in_b_sb[:, 0:1]).then_inc(work_read, 1)
                        if scan:
                            decays(1, c, 11, 22)
                    if k == 4 and scan:
                        decays(1, c, 22, N)
                    if k == 7 and prep:
                        q = c + 1
                        full("z", c)
                        if later or q >= 2:
                            act.wait_ge(yz_done, q - 1)
                        settle()
                        nc.scalar.activation(z_act[:, q % 2, :], work[:, :], ACT.Silu,
                                             bias=in_b_sb[:, 1:2]).then_inc(work_read, 1)
                        act.wait_ge(conv_step, 2 * K * q + 2 * K - 1)
                        if later or q >= 1:
                            act.wait_ge(work_full, work_count("c1", c))
                            act.wait_ge(dtx_done, q)
                        nc.scalar.activation(xs[:, :], cv[:, :], ACT.Silu, bias=conv_b_sb[:, 0:1]).then_inc(xs_done, 1)
                    if k == 8 and prep:
                        q = c + 1
                        act.preload_act_table_set("natural_log_exp_and_others")
                        act.wait_ge(work_read, work_count("dt", c))
                        nc.scalar.activation(dt_exp[:, :], dt_raw[:, :], ACT.Exp).then_inc(dt_exp_done, 1)
                        act.wait_ge(dt_exp_done, q + 1)
                        nc.scalar.activation(dt_raw[:, :], dt_exp[:, :], ACT.Ln, bias=1.0).then_inc(dt_log_done, 1)
                    if k == 9 and prep:
                        decays(0, c + 1, 0, 11)
                    if k == 10 and prep:
                        full("dtx0", c)
                        if later or c >= 0:
                            act.wait_ge(input_made, T * c + HT)
                        nc.scalar.activation(dtx_tok[:, 0:NT // 2, :],
                                             work[:, 0:TOK // 2].rearrange("p (j d) -> p j d", d=D),
                                             ACT.Copy).then_inc(work_read, 1)
                    if k == 12 and prep:
                        decays(0, c + 1, 11, 22)
                    if k == 13 and prep:
                        decays(0, c + 1, 22, N)
                    if k == 15 and post:
                        q = c - 1
                        full("turn2", c)
                        nc.scalar.activation(h2_t[:, :], work[:, :], ACT.Copy).then_inc(work_read, 1)
                        act.wait_ge(gap_done, q + 1)
                        nc.scalar.activation(rt[:, 1, :], rt[:, 0, :], ACT.Exp).then_inc(gap_exp, 1)

            macros(act, body)

        @block.vector
        def _(dve):
            nc.vector.memset(x_in[:, NT, :], 0.0).then_inc(set_up, 1)
            dve.wait_ge(params_in, 16 * len(params))
            nc.vector.tensor_scalar(neg_a[:, :], neg_a[:, :], -5.0, 2.0, ALU.max, ALU.min).then_inc(set_up, 1)
            nc.vector.memset(edge[:, :], 1.0).then_inc(set_up, 1)
            nc.vector.memset(group_mask[:, :], 0.0).then_inc(set_up, 1)
            dve.wait_ge(set_up, 4)
            nc.vector.memset(edge[:, CH - 1:CH], 0.0).then_inc(set_up, 1)
            for i in range(BQ):
                nc.vector.memset(group_mask[i * N:(i + 1) * N, i:i + 1], 1.0).then_inc(set_up, 1)
            nc.vector.memset(eps_t[:, :], EPS).then_inc(set_up, 1)
            nc.vector.memset(minus_half[:, :], -0.5).then_inc(set_up, 1)
            nc.vector.memset(zero_t[:, :], 0.0).then_inc(set_up, 1)
            nc.vector.memset(xc[:, 0:2 * NB], 0.0).then_inc(set_up, 1)
            nc.vector.memset(state[:, 1, :], 0.0).then_inc(set_up, 1)
            for e in range(E):
                nc.vector.memset(iota_e[:, 0, e:e + 1], float(e)).then_inc(set_up, 1)
            n = 4 + 1 + BQ + 5 + E
            dve.wait_ge(a_exp, 1)
            nc.vector.tensor_scalar(neg_a[:, :], neg_a[:, :], -1.0, None, ALU.mult).then_inc(set_up, 1)
            n += 1
            dve.wait_ge(mod_ready, 1)
            sa, ca, ga, sb_ = (up_ps[0][:, i * D:(i + 1) * D] for i in range(4))
            cb, gb = (up_ps[1][:, i * D:(i + 1) * D] for i in range(2))
            nc.vector.tensor_copy(shift_a[:, 0, :], sa).then_inc(set_up, 1)
            nc.vector.tensor_scalar(scale_a[:, 0, :], ca, 1.0, None, ALU.add).then_inc(set_up, 1)
            nc.vector.tensor_copy(shift_b[:, 0, :], sb_).then_inc(set_up, 1)
            nc.vector.tensor_scalar(scale_b[:, 0, :], cb, 1.0, None, ALU.add).then_inc(set_up, 1)
            n += 4
            for g, dst in ((ga, gate_t[:, 3, :]), (gb, gate_b[:, 0, :])):
                dve.wait_ge(set_up, n)
                nc.vector.tensor_scalar(gate_t[:, 0, :], g, -1.0, None, ALU.mult).then_inc(set_up, 1)
                nc.vector.tensor_scalar(gate_t[:, 1, :], g, 0.0, 2.0, ALU.is_ge, ALU.mult).then_inc(set_up, 1)
                dve.wait_ge(set_up, n + 2)
                nc.vector.tensor_tensor(gate_t[:, 0, :], g, gate_t[:, 0, :], ALU.max).then_inc(set_up, 1)
                nc.vector.tensor_scalar(gate_t[:, 1, :], gate_t[:, 1, :], -1.0, None, ALU.add).then_inc(set_up, 1)
                dve.wait_ge(set_up, n + 4)
                nc.vector.scalar_tensor_tensor(out=dst, in0=gate_t[:, 0, :], scalar=GATE_MIN, in1=gate_t[:, 1, :],
                                               op0=ALU.max, op1=ALU.mult).then_inc(set_up, 1)
                n += 5
            dve.wait_ge(set_up, n)
            nc.vector.tensor_tensor(gate_g[:, 0, :], gate_t[:, 3, :], g_row[:, :], ALU.mult).then_inc(set_up, 1)
            dve.wait_ge(set_up, n + 1)
            nc.vector.tensor_tensor(gate_beta[:, 0, :], gate_t[:, 3, :], beta_row[:, :], ALU.mult).then_inc(started, 1)

            def settle():
                dve.wait_ge(started, 1)

            def moments(src, bn, mv, tiles, mv_done):
                for j in range(tiles):
                    nc.vector.bn_stats(bn[:, j, :], src[:, j, :])
                nc.vector.drain()
                for j in range(tiles):
                    nc.vector.bn_aggr(mv[:, j, :], bn[:, j, :]).then_inc(mv_done, 1)

            def normalise(dst, src, mv, rstd, tiles, done):
                for j in range(tiles):
                    nc.vector.tensor_scalar(dst[:, j, :], src[:, j, :], mv[:, j, 0:1], rstd[:, j:j + 1],
                                            ALU.subtract, ALU.mult).then_inc(done, 1)

            def full(name, c):
                dve.wait_ge(work_full, work_count(name, c))

            def c_diagonal(half):
                nc.vector.scalar_tensor_tensor(
                    out=c_diag[:, half * TOK // 2:(half + 1) * TOK // 2].rearrange("p (g b) -> p g b", b=BQ),
                    in0=work[:, 0:TOK // 2].rearrange("p (g b) -> p g b", b=BQ), scalar=c_b_col[:, 0:1],
                    in1=group_mask[:, :].unsqueeze(1).broadcast_to([P, HT * BG, BQ]),
                    op0=ALU.add, op1=ALU.mult).then_inc(work_read, 1)

            def scan_step(k, c):
                n = T * c + k
                dve.wait_ge(decay_turned, n + 1)
                if not isinstance(c, int) or n >= 1:
                    dve.wait_ge(state_done, n)
                nc.vector.tensor_tensor(prod[:, :], decay_ps[:, :, :].rearrange("p g d -> p (g d)"),
                                        state[:, (k + 1) % 2, :], ALU.mult).then_inc(decayed, 1)
                dve.wait_ge(input_made, n + 1)
                dve.wait_ge(decayed, n + 1)
                nc.vector.tensor_tensor(total[:, :], input_ps[:, :, :].rearrange("p g d -> p (g d)"), prod[:, :],
                                        ALU.add).then_inc(added, 1)
                dve.wait_ge(added, n + 1)
                if not isinstance(c, int) or n >= 2:
                    dve.wait_ge(y_done, n - 1)
                nc.vector.tensor_scalar(state[:, k % 2, :], total[:, :], -CLIP, CLIP, ALU.max,
                                        ALU.min).then_inc(state_done, 1)

            def body(c):
                prep, scan, post, ffn = (active(s, c) for s in STAGES)
                later = not isinstance(c, int)
                for k in range(T):
                    if scan:
                        scan_step(k, c)
                    if k == 0:
                        if scan:
                            full("c1", c)
                            if later or c >= 1:
                                dve.wait_ge(y_done, T * c)
                            c_diagonal(1)
                        if post:
                            q = c - 1
                            dve.wait_ge(y_done, T * (q + 1))
                            if later or q >= 1:
                                dve.wait_ge(work_full, work_count("proj", c - 1))
                            settle()
                            nc.vector.tensor_tensor(yz[:, :], y_ps[:, :], z_act[:, q % 2, :], ALU.mult).then_inc(yz_done, 1)
                        if prep:
                            q = c + 1
                            dve.wait_ge(x_loaded, LOADS * (q + 1))
                            moments(x_in, bn1, mv1, NT + 1, mv1_done)
                    if k == 1:
                        if post:
                            q = c - 1
                            full("proj", c)
                            dve.wait_ge(h_res_done, q + 1)
                            if later or q >= 1:
                                dve.wait_ge(x2_step, 3 * q)
                            settle()
                            nc.vector.tensor_tensor(o[:, :, :].rearrange("p j d -> p (j d)"), work[:, :],
                                                    h_res[:, q % 2, :], ALU.add).then_inc(work_read, 1)
                        if prep:
                            q = c + 1
                            dve.wait_ge(rstd1_done, q + 1)
                            if later or q >= 1:
                                dve.wait_ge(h_scaled, q)
                            normalise(xn, x_in, mv1, rstd1, NT + 1, xn_done)
                        if post:
                            dve.wait_ge(work_read, work_count("proj", c))
                            moments(o, bn2, mv2, NT, mv2_done)
                    if k == 2 and post:
                        q = c - 1
                        dve.wait_ge(rstd2_done, q + 1)
                        normalise(o, o, mv2, rstd2, NT, on_done)
                    if k == 4:
                        if prep:
                            q = c + 1
                            full("xc_next", c)
                            if later or q >= 1:
                                dve.wait_ge(conv_step, 2 * K * q)
                            nc.vector.tensor_scalar(xc[:, 2 * NB + TOK:], work[:, 0:NB], in_b_sb[:, 0:1],
                                                    edge[:, q:q + 1] if isinstance(q, int) else edge_col(q), ALU.add, ALU.mult)\
                              .then_inc(work_read, 1)
                        if post:
                            q = c - 1
                            dve.wait_ge(x2_step, 3 * (q + 1))
                            moments(x2, bn3, mv3, NT, mv3_done)
                    if k == 6 and post:
                        q = c - 1
                        dve.wait_ge(rstd3_done, q + 1)
                        if later or q >= 1:
                            dve.wait_ge(work_full, work_count("turn2", c - 1))
                        normalise(h2, x2, mv3, rstd3, NT, n2_done)
                    if k == 8 and prep:
                        q = c + 1
                        full("dt", c)
                        if later or q >= 1:
                            dve.wait_ge(dt_done, q)
                        nc.vector.tensor_scalar(dt_raw[:, :], work[:, :], dt_b_sb[:, 0:1], DT_IN_MAX, ALU.add,
                                                ALU.min).then_inc(work_read, 1)
                        full("b", c)
                        if later or q >= 1:
                            dve.wait_ge(b_diag_done, NT * q)
                        nc.vector.tensor_tensor(b_tok[:, :, :], work[:, 0:NT * N].rearrange("p (j n) -> p j n", n=N),
                                                b_b_row[:, :, :].broadcast_to([P, NT, N]), ALU.add).then_inc(work_read, 1)
                    if k == 9 and prep:
                        q = c + 1
                        dve.wait_ge(dt_log_done, q + 1)
                        if later or q >= 1:
                            dve.wait_ge(decay_made[1], N * q)
                            dve.wait_ge(dtx_done, q)
                        nc.vector.tensor_scalar(dt[:, :], dt_raw[:, :], DT_MIN, DT_MAX, ALU.max, ALU.min).then_inc(dt_done, 1)
                        full("c0", c)
                        if later or q >= 1:
                            dve.wait_ge(y_done, T * c + HT)
                        c_diagonal(0)
                    if ffn:
                        for e in range(EX):
                            if DOWN_AT[e] == k:
                                q = c - 2
                                full(f"down{e}", c)
                                if e == 0:
                                    if later or q >= 1:
                                        dve.wait_ge(final_step, 2 * q)
                                    nc.vector.tensor_copy(acc[:, :, :], work[:, :].rearrange("p (j d) -> p j d", d=D))\
                                      .then_inc(work_read, 1)
                                else:
                                    if e >= 3:
                                        dve.wait_ge(acc_step, E * q + e - 2)
                                    nc.vector.tensor_tensor(
                                        scaled[:, e % 2, :].rearrange("p (j d) -> p j d", d=D),
                                        work[:, :].rearrange("p (j d) -> p j d", d=D),
                                        cw[:, :, e - 1:e].broadcast_to([P, NT, D]), ALU.mult).then_inc(work_read, 1)
                    if k == 15 and post:
                        route(c, c - 1)

            def edge_col(q):
                return edge[:, :].rearrange("p (c o) -> p c o", o=1)[:, q, :]

            def route(c, q):
                full("logits", c)
                nc.vector.tensor_copy(lg[:, :, :], work[:, 0:NT * E].rearrange("p (j e) -> p j e", e=E)).then_inc(work_read, 1)
                nc.vector.drain()
                for j in range(NT):
                    nc.vector.max(top_v[:, j, :], lg[:, j, :])
                nc.vector.drain()
                for j in range(NT):
                    nc.vector.max_index(top_i[:, j, :], top_v[:, j, :], lg[:, j, :]).then_inc(index_done, 1)
                nc.vector.tensor_tensor(rt[:, 0, :], top_v[:, :, 1], top_v[:, :, 0], ALU.subtract).then_inc(gap_done, 1)
                dve.wait_ge(index_done, NT * (q + 1))
                nc.vector.tensor_copy(top_f[:, :, :], top_i[:, :, 0:2]).then_inc(route_step, 1)
                dve.wait_ge(gap_exp, q + 1)
                n = 9 * q
                nc.vector.tensor_scalar(rt[:, 2, :], rt[:, 1, :], 1.0, None, ALU.add).then_inc(route_step, 1)
                dve.wait_ge(route_step, n + 2)
                nc.vector.reciprocal(rt[:, 3, :], rt[:, 2, :]).then_inc(route_step, 1)
                dve.wait_ge(route_step, n + 3)
                nc.vector.tensor_tensor(rt[:, 2, :], rt[:, 1, :], rt[:, 3, :], ALU.mult).then_inc(route_step, 1)
                for i in range(2):
                    nc.vector.tensor_tensor(pick[:, i, :, :], iota_e[:, :, :].broadcast_to([P, NT, E]),
                                            top_f[:, :, i:i + 1].broadcast_to([P, NT, E]), ALU.is_equal).then_inc(route_step, 1)
                dve.wait_ge(route_step, n + 6)
                for i, share in enumerate((3, 2)):
                    nc.vector.tensor_tensor(pick[:, i, :, :], pick[:, i, :, :],
                                            rt[:, share, :].unsqueeze(2).broadcast_to([P, NT, E]), ALU.mult).then_inc(route_step, 1)
                dve.wait_ge(route_step, n + 8)
                nc.vector.tensor_tensor(cw[:, :, :], pick[:, 0, :, :], pick[:, 1, :, :], ALU.add).then_inc(route_step, 1)

            macros(dve, body)

        @block.tensor
        def _(pe):
            pe.wait_ge(cond_ready, 1)
            nc.tensor.matmul(up_ps[0][:, :], cond[:, :], wmod_sb[:, 0:4 * D], start=True, stop=True)
            nc.tensor.matmul(up_ps[1][:, 0:2 * D], cond[:, :], wmod_sb[:, 4 * D:], start=True, stop=True).then_inc(mod_ready, 1)
            pe.wait_ge(started, 1)
            pe.wait_ge(diag_set, 1)

            def free_work(name, c):
                count = work_count(name, c) - 1
                if not isinstance(c, int) or count >= 1:
                    pe.wait_ge(work_read, count)

            def turn_decays(k, q):
                n = T * q + k
                if k % HT == 0:
                    pe.wait_ge(decay_made[k // HT], N * (q + 1))
                if not isinstance(q, int) or n >= 1:
                    pe.wait_ge(decayed, n)
                for g in range(BG):
                    last = nc.tensor.transpose(decay_ps[:, g, :],
                                               decay[:, k, g * BQ:(g + 1) * BQ, :].rearrange("p b n -> p (b n)"), ident[:, :])
                last.then_inc(decay_turned, 1)

            def make_inputs(k, q):
                n = T * q + k
                j, t = k // SPT, k % SPT
                if t == 0:
                    pe.wait_ge(b_diag_done, NT * q + j + 1)
                if k == 0:
                    pe.wait_ge(work_read, work_count("dtx0", q - 1))
                if k == HT:
                    pe.wait_ge(work_read, work_count("dtx1", q))
                if not isinstance(q, int) or n >= 1:
                    pe.wait_ge(added, n)
                for g in range(BG):
                    last = nc.tensor.matmul(
                        input_ps[:, g, :],
                        b_diag[rows(t), j % 2, g * BQ:(g + 1) * BQ, :].rearrange("p b n -> p (b n)"),
                        dtx_tok[rows(t), j, :], start=True, stop=True)
                last.then_inc(input_made, 1)

            def read_out(k, q):
                n = T * q + k
                pe.wait_ge(state_done, n + 1)
                if k == 0:
                    pe.wait_ge(work_read, work_count("c0", q - 1))
                    if not isinstance(q, int) or q >= 1:
                        pe.wait_ge(yz_done, q)
                if k == HT:
                    pe.wait_ge(work_read, work_count("c1", q))
                for g in range(BG):
                    col = k * NB + g * BQ
                    last = nc.tensor.matmul(y_ps[:, col:col + BQ], state[:, k % 2, g * D:(g + 1) * D],
                                            c_diag[:, col:col + BQ], start=True, stop=True)
                last.then_inc(y_done, 1)

            def turn(src, tiles):
                for i, j in enumerate(tiles):
                    last = nc.tensor.transpose(work[:, i * P:(i + 1) * P], src(j), ident[:, :])
                return last

            def use(name, c):
                free_work(name, c)
                if name in ("dtx0", "dtx1"):
                    q = c + 1 if name == "dtx0" else c
                    pe.wait_ge(dtx_done, q + 1)
                    half = int(name[-1]) * NT // 2
                    last = turn(lambda j: dtx[:, j * P:(j + 1) * P], range(half, half + NT // 2))
                elif name in ("c0", "c1"):
                    q = c + 1 if name == "c0" else c
                    pe.wait_ge(xs_done, q + 1)
                    half = int(name[-1]) * TOK // 2
                    last = nc.tensor.matmul(work[:, 0:TOK // 2], c_w_sb[:, :], xs[:, half:half + TOK // 2], start=True, stop=True)
                elif name == "turn":
                    pe.wait_ge(h_done, c + 2)
                    last = turn(lambda j: h[:, j, :], range(NT))
                elif name == "turn_next":
                    last = turn(lambda j: h[:, j, :], [NT])
                elif name == "xc":
                    last = nc.tensor.matmul(work[:, :], in_w_sb[:, 0:D], h_t[:, 0:TOK], start=True, stop=True)
                elif name == "xc_next":
                    last = nc.tensor.matmul(work[:, 0:NB], in_w_sb[:, 0:D], h_t[:, TOK:], start=True, stop=True)
                elif name == "z":
                    last = nc.tensor.matmul(work[:, :], in_w_sb[:, D:], h_t[:, 0:TOK], start=True, stop=True)
                elif name == "dt":
                    pe.wait_ge(xs_done, c + 2)
                    last = nc.tensor.matmul(work[:, :], dt_w_sb[:, :], xs[:, :], start=True, stop=True)
                elif name == "b":
                    for j in range(NT):
                        last = nc.tensor.matmul(work[:, j * N:(j + 1) * N], xs[:, j * P:(j + 1) * P], b_w_sb[:, :],
                                                start=True, stop=True)
                elif name == "proj":
                    pe.wait_ge(yz_done, c)
                    for j in range(NT):
                        last = nc.tensor.matmul(work[:, j * D:(j + 1) * D], yz[:, j * P:(j + 1) * P], out_w_sb[:, :],
                                                start=True, stop=True)
                elif name == "turn2":
                    pe.wait_ge(h2_step, 2 * c)
                    last = turn(lambda j: h2[:, j, :], range(NT))
                elif name == "logits":
                    for j in range(NT):
                        last = nc.tensor.matmul(work[:, j * E:(j + 1) * E], h2_t[:, j * P:(j + 1) * P], wg_sb[:, :],
                                                start=True, stop=True)
                else:
                    e = int(name[4:])
                    for f in range(FT):
                        pe.wait_ge(gelu_done[f], EX * (c - 2) + e + 1)
                    for j in range(NT):
                        for f in range(FT):
                            last = nc.tensor.matmul(work[:, j * D:(j + 1) * D], hid[:, e % HBUF, f, j * P:(j + 1) * P],
                                                    wd_sb[:, e, f, :], start=(f == 0), stop=(f == FT - 1))
                last.then_inc(work_full, 1)

            def uses(k, place, c):
                for where, stage, name in at_step(k):
                    if where == place and active(stage, c):
                        use(name, c)

            def up(e, q):
                for f in range(FT):
                    if e >= 1 or not isinstance(q, int) or q >= 1:
                        pe.wait_ge(gelu_done[f], EX * q + e)
                    nc.tensor.matmul(up_ps[f][:, :], wu_sb[:, e, f * P:(f + 1) * P], h2_t[:, :], start=True, stop=True)\
                      .then_inc(up_done[f], 1)

            def body(c):
                prep, scan, post, ffn = (active(s, c) for s in STAGES)
                for k in range(T):
                    uses(k, "a", c)
                    if k > 0 and scan:
                        read_out(k - 1, c)
                    elif k == 0 and active("scan", c - 1 if isinstance(c, int) else c):
                        read_out(T - 1, c - 1)
                    if ffn:
                        if k == 0:
                            if isinstance(c, int) and c == 2:
                                pe.wait_ge(ffn_in, 32)
                            pe.wait_ge(work_read, work_count("turn2", c - 1))
                        for e in range(EX):
                            if UP_AT[e] == k:
                                up(e, c - 2)
                    uses(k, "b", c)
                    if k < T - 1 and scan:
                        turn_decays(k + 1, c)
                        make_inputs(k + 1, c)
                    elif k == T - 1 and prep:
                        turn_decays(0, c + 1)
                        make_inputs(0, c + 1)
                    uses(k, "c", c)

            macros(pe, body)


_INS = ["x", "in_w", "in_b", "conv_w", "conv_b", "a_log", "b_w", "b_b", "c_w", "c_b", "dt_w", "dt_b", "out_w",
        "out_b", "ln_g", "ln_beta", "wg", "wu", "wd", "c_t", "wmod"]


def kernel(**inputs):
    import concourse.bacc as _bacc
    from concourse.bass_utils import run_bass_kernel_spmd as _run

    g = {name[3:]: np.asarray(a) for name, a in inputs.items()}

    def rows_of(v):
        return np.broadcast_to(v, (P, v.shape[0]))

    laid = {
        "x": g["attn_x"],
        "in_w": g["attn_in_proj_w"].T,
        "in_b": g["attn_in_proj_b"].reshape(2, D).T,
        "conv_w": g["attn_conv_w"].reshape(D, K),
        "conv_b": g["attn_conv_b"].reshape(D, 1),
        "a_log": g["attn_A_log"],
        "b_w": g["attn_B_w"].T,
        "b_b": rows_of(g["attn_B_b"]),
        "c_w": np.tile(g["attn_C_w"].T, (1, BQ)),
        "c_b": np.tile(g["attn_C_b"], BQ).reshape(P, 1),
        "dt_w": g["attn_dt_w"].T,
        "dt_b": g["attn_dt_b"].reshape(D, 1),
        "out_w": g["attn_out_w"].T,
        "out_b": rows_of(g["attn_out_b"]),
        "ln_g": rows_of(g["attn_ln_g"]),
        "ln_beta": rows_of(g["attn_ln_beta"]),
        "wg": g["ffn_Wg"],
        "wu": np.concatenate([g["ffn_W1"][None], g["ffn_Wu"]]).transpose(1, 0, 2),
        "wd": np.concatenate([g["ffn_W2"][None], g["ffn_Wd"]]).reshape(EX, FT, P, D).transpose(2, 0, 1, 3),
        "c_t": np.tile(g["c"].T, (1, SPT)),
        "wmod": g["wmod"],
    }
    nc = _bacc.Bacc("TRN2", target_bir_lowering=False, num_devices=1)
    arrays, args = {}, []
    for name in _INS:
        a = np.ascontiguousarray(laid[name])
        arrays[f"in_{name}"] = a
        args.append(nc.dram_tensor(f"in_{name}", a.shape, mybir.dt.from_np(a.dtype), kind="ExternalInput").ap())
    args.append(nc.dram_tensor("out_y", (NB, L, D), F32, kind="ExternalOutput").ap())
    adaln_block(nc, *args)
    r = _run(nc, [arrays], core_ids=[0])
    return r.results[0]["out_y"]
```

```python
from contextlib import ExitStack

import numpy as np

import concourse.bass as bass
from concourse import mybir

F32 = mybir.dt.float32
BF16 = mybir.dt.bfloat16
U32 = mybir.dt.uint32
ALU = mybir.AluOpType
ACT = mybir.ActivationFunctionType

NB, L, D, N, K = 32, 256, 128, 32, 4
F, E, MOD = 256, 8, 6
P = 128
T = 16
TOK = T * NB
NT = TOK // P
SPT = P // NB
CH = L // T
BQ = P // N
BG = NB // BQ
HT = T // 2
FT = F // P
EX = E + 1
PARTS = 3
GV = 4
HBUF = 3
CLIP, EPS = 10.0, 1e-5
DT_MIN, DT_MAX, DT_IN_MAX = 0.001, 0.2, 20.0
GATE_MIN = 0.25

UP_AT = (0, 0, 1, 5, 5, 6, 10, 10, 11)
DOWN_AT = (1, 2, 3, 6, 7, 8, 11, 12, 13)

WORK = [
    (0, "a", "scan", "dtx1"), (0, "b", "scan", "c1"), (0, "c", "post", "turn_y"),
    (1, "b", "post", "proj"), (1, "c", "ffn", "down0"),
    (2, "a", "prep", "turn"), (2, "b", "prep", "turn_next"), (2, "c", "ffn", "down1"),
    (3, "a", "prep", "xc"), (3, "c", "ffn", "down2"),
    (4, "a", "prep", "xc_next"),
    (6, "c", "ffn", "down3"),
    (7, "a", "prep", "z"), (7, "c", "ffn", "down4"),
    (8, "a", "prep", "dt"), (8, "b", "prep", "b"), (8, "c", "ffn", "down5"),
    (9, "a", "prep", "c0"),
    (10, "a", "prep", "dtx0"),
    (11, "c", "ffn", "down6"), (12, "c", "ffn", "down7"), (13, "c", "ffn", "down8"),
    (15, "a", "post", "turn2"), (15, "c", "post", "logits"),
]
STAGES = ("prep", "scan", "post", "ffn")
LAG = {"prep": -1, "scan": 0, "post": 1, "ffn": 2}
USES = {s: sum(u[2] == s for u in WORK) for s in STAGES}
FULL_FROM, FULL_TO = 2, CH - 2
LOOP_FROM, LOOP_TO = FULL_FROM + 1, CH - 1


def active(stage, c):
    return not isinstance(c, int) or 0 <= c - LAG[stage] < CH


def work_before(c):
    if isinstance(c, int):
        return sum(USES[s] * min(max(c - LAG[s], 0), CH) for s in STAGES)
    return c * sum(USES.values()) - sum(USES[s] * LAG[s] for s in STAGES)


def work_count(name, c):
    n = 0
    for _, _, stage, use in WORK:
        n += active(stage, c)
        if use == name:
            return work_before(c) + n
    raise KeyError(name)


def macros(eng, body, loop_to=LOOP_TO):
    for c in range(-1, LOOP_FROM):
        body(c)
    with eng.Fori(LOOP_FROM, loop_to) as c:
        body(c)
    for c in range(loop_to, CH + 2):
        body(c)


def adaln_block(nc, x, in_w, in_b, conv_w, conv_b, a_log, b_w, b_b, c_w, c_b, dt_w, dt_b, out_w, out_b,
                ln_g, ln_beta, wg, wu, wd, c_t, wmod, out):
    ctx = ExitStack()
    with ctx:
        def sb(name, shape, dt=F32):
            return ctx.enter_context(nc.sbuf_tensor(name, shape, dt))

        def ps(name, shape):
            return ctx.enter_context(nc.psum_tensor(name, shape, F32))

        def sem(name):
            return ctx.enter_context(nc.semaphore(name))

        in_w_sb = sb("in_w_sb", [P, 2 * D])
        dt_w_sb = sb("dt_w_sb", [P, D])
        b_w_sb = sb("b_w_sb", [P, BQ * N])
        c_w_sb = sb("c_w_sb", [P, BQ * N])
        out_w_sb = sb("out_w_sb", [P, D])
        wg_sb = sb("wg_sb", [P, E])
        wu_sb = sb("wu_sb", [P, EX, F])
        wd_sb = sb("wd_sb", [P, EX, FT, D])
        cond = sb("cond", [P, P])
        in_b_sb = sb("in_b_sb", [P, 2])
        conv_w_sb = sb("conv_w_sb", [P, K])
        conv_b_sb = sb("conv_b_sb", [P, 1])
        neg_a = sb("neg_a", [P, N])
        b_b_col = sb("b_b_col", [P, 1])
        c_b_col = sb("c_b_col", [P, 1])
        dt_b_sb = sb("dt_b_sb", [P, 1])
        out_b_row = sb("out_b_row", [P, 1, D])
        g_row = sb("g_row", [P, D])
        beta_row = sb("beta_row", [P, D])
        ident = sb("ident", [P, P])
        shift_a = sb("shift_a", [P, 1, D])
        scale_a = sb("scale_a", [P, 1, D])
        gate_g = sb("gate_g", [P, 1, D])
        gate_beta = sb("gate_beta", [P, 1, D])
        shift_b = sb("shift_b", [P, 1, D])
        scale_b = sb("scale_b", [P, 1, D])
        gate_b = sb("gate_b", [P, 1, D])
        spread = sb("spread", [PARTS * NB, NB, N], BF16)
        group_mask = sb("group_mask", [P, BQ])
        ident_b = sb("ident_b", [P, P], BF16)
        edge = sb("edge", [P, CH])
        eps_t = sb("eps_t", [P, 1])
        minus_half = sb("minus_half", [P, 1])
        zero_t = sb("zero_t", [P, 1])
        iota_e = sb("iota_e", [P, 1, E])

        x_in = sb("x_in", [P, NT + 1, D])
        bn1 = sb("bn1", [P, NT + 1, 6])
        mv1 = sb("mv1", [P, NT + 1, 2])
        ve1 = sb("ve1", [P, NT + 1])
        rstd1 = sb("rstd1", [P, NT + 1])
        h = sb("h", [P, NT + 1, D])
        h_res = sb("h_res", [P, 2, TOK])
        h_t = sb("h_t", [P, TOK + NB])
        xc = sb("xc", [P, (T + K - 1) * NB])
        cv = sb("cv", [P, TOK])
        xs = sb("xs", [P, TOK])
        z_act = sb("z_act", [P, 2, TOK])
        dt_raw = sb("dt_raw", [P, TOK])
        dt = sb("dt", [P, TOK])
        dtx = sb("dtx", [P, TOK])
        scratch = sb("scratch", [P, TOK])
        dtx_part = sb("dtx_part", [P, T, PARTS, NB], BF16)
        dtx_rows = sb("dtx_rows", [PARTS * NB, T, D], BF16)
        b_q = sb("b_q", [P, 2, T * BG])
        c_diag = sb("c_diag", [P, T, BG, NB + BQ])
        decay = sb("decay", [P, T, NB, N])
        state = sb("state", [P, 2, BG * D])
        scaled_in = sb("scaled_in", [P, 2, BG, D])
        prod = sb("prod", [P, BG * D])
        y_tok = sb("y_tok", [P, NT, D])
        yz = sb("yz", [P, TOK])
        o = sb("o", [P, NT, D])
        bn2 = sb("bn2", [P, NT, 6])
        mv2 = sb("mv2", [P, NT, 2])
        ve2 = sb("ve2", [P, NT])
        rstd2 = sb("rstd2", [P, NT])
        x_res = sb("x_res", [P, NT, D])
        x2 = sb("x2", [P, NT, D])
        bn3 = sb("bn3", [P, NT, 6])
        mv3 = sb("mv3", [P, NT, 2])
        ve3 = sb("ve3", [P, NT])
        rstd3 = sb("rstd3", [P, NT])
        h2 = sb("h2", [P, NT, D])
        h2_t = sb("h2_t", [P, TOK])
        lg = sb("lg", [P, NT, E])
        top_v = sb("top_v", [P, NT, 8])
        top_i = sb("top_i", [P, NT, 8], U32)
        top_f = sb("top_f", [P, NT, 2])
        rt = sb("rt", [P, 4, NT])
        pick = sb("pick", [P, 2, NT, E])
        cw = sb("cw", [P, NT, E])
        hid = sb("hid", [P, HBUF, FT, TOK])
        wmod_sb = hid[:, 0, :, :].rearrange("p f t -> p (f t)")[:, 0:MOD * D]
        gate_t = hid[:, 1, 0, :].rearrange("p (i d) -> p i d", i=4)
        scaled = sb("scaled", [P, 2, TOK])
        acc = sb("acc", [P, NT, D])
        x2_keep = sb("x2_keep", [P, NT, D])

        decay_ps = ps("decay_ps", [P, BG, D])
        input_ps = ps("input_ps", [P, BG, D])
        y_ps = ps("y_ps", [P, NT, D])
        up_ps = [ps(f"up_ps{f}", [P, TOK]) for f in range(FT)]
        work = ps("work", [P, TOK])

        params_in = sem("params_in")
        ffn_in = sem("ffn_in")
        ident_set = sem("ident_set")
        diag_set = sem("diag_set")
        consts_set = sem("consts_set")
        cond_ready = sem("cond_ready")
        mod_ready = sem("mod_ready")
        set_up = sem("set_up")
        a_exp = sem("a_exp")
        started = sem("started")
        work_full = sem("work_full")
        work_read = sem("work_read")
        x_loaded = sem("x_loaded")
        mv1_done = sem("mv1_done")
        ve1_done = sem("ve1_done")
        rstd1_done = sem("rstd1_done")
        xn_done = sem("xn_done")
        h_scaled = sem("h_scaled")
        h_done = sem("h_done")
        h_res_done = sem("h_res_done")
        conv_step = sem("conv_step")
        xs_done = sem("xs_done")
        dt_exp_done = sem("dt_exp_done")
        dt_log_done = sem("dt_log_done")
        dt_done = sem("dt_done")
        dtx_done = sem("dtx_done")
        parts_step = sem("parts_step")
        decay_made = [sem("decay_made0"), sem("decay_made1")]
        decay_turned = sem("decay_turned")
        input_made = sem("input_made")
        scaled_v = sem("scaled_v")
        scaled_a = sem("scaled_a")
        decayed = sem("decayed")
        added = sem("added")
        state_done = sem("state_done")
        y_done = sem("y_done")
        y_kept = sem("y_kept")
        x_res_loaded = sem("x_res_loaded")
        mv2_done = sem("mv2_done")
        ve2_done = sem("ve2_done")
        rstd2_done = sem("rstd2_done")
        on_done = sem("on_done")
        x2_step = sem("x2_step")
        mv3_done = sem("mv3_done")
        ve3_done = sem("ve3_done")
        rstd3_done = sem("rstd3_done")
        n2_done = sem("n2_done")
        h2_step = sem("h2_step")
        index_done = sem("index_done")
        gap_done = sem("gap_done")
        gap_exp = sem("gap_exp")
        route_step = sem("route_step")
        up_done = [sem(f"up_done{f}") for f in range(FT)]
        gelu_done = [sem(f"gelu_done{f}") for f in range(FT)]
        acc_step = sem("acc_step")
        kept = sem("kept")
        final_step = sem("final_step")
        stored = sem("stored")

        block = ctx.enter_context(nc.Block())

        params = [(in_w_sb[:, :], in_w), (in_b_sb[:, :], in_b), (conv_w_sb[:, :], conv_w), (conv_b_sb[:, :], conv_b),
                  (neg_a[:, :], a_log), (b_w_sb[:, :], b_w), (b_b_col[:, :], b_b), (c_w_sb[:, :], c_w),
                  (c_b_col[:, :], c_b), (dt_w_sb[:, :], dt_w), (dt_b_sb[:, :], dt_b), (out_w_sb[:, :], out_w),
                  (out_b_row[:, 0, :], out_b), (g_row[:, :], ln_g), (beta_row[:, :], ln_beta), (wg_sb[:, :], wg),
                  (cond[:, :], c_t), (wmod_sb[:, :], wmod)]
        x_steps = x.rearrange("b (c j t) d -> c t b j d", c=CH, t=SPT)
        out_steps = out.rearrange("b (c j t) d -> c t b j d", c=CH, t=SPT)
        LOADS = 16 * (SPT + 1)
        MOVES = 16 * SPT

        def rows(t):
            return slice(t * NB, (t + 1) * NB)

        def at_step(k):
            return [u[1:] for u in WORK if u[0] == k]

        @block.sync
        def _(sp):
            def load_x(q):
                for t in range(SPT):
                    sp.dma_start(x_in[rows(t), 0:NT, :], x_steps[q, t]).then_inc(x_loaded, 16)
                ahead = min(q + 1, CH - 1) if isinstance(q, int) else q + 1
                sp.dma_start(x_in[rows(0), NT, :], x_steps[ahead, 0][:, 0, :]).then_inc(x_loaded, 16)

            for i, (dst, src) in enumerate(params):
                if i % 2 == 0:
                    sp.dma_start(dst, src).then_inc(params_in, 16)
            sp.wait_ge(set_up, 1)
            load_x(0)
            sp.dma_start(wu_sb[:, :, :], wu).then_inc(ffn_in, 16)
            sp.dma_start(wd_sb[:, :, :, :], wd).then_inc(ffn_in, 16)

            def body(c):
                if active("prep", c) and (not isinstance(c, int) or c + 2 < CH):
                    sp.wait_ge(xn_done, (NT + 1) * (c + 2))
                    load_x(c + 2)
                if active("scan", c):
                    if not isinstance(c, int) or c >= 1:
                        sp.wait_ge(x2_step, 3 * c)
                    for t in range(SPT):
                        sp.dma_start(x_res[rows(t), :, :], x_steps[c, t]).then_inc(x_res_loaded, 16)
                if active("ffn", c):
                    sp.wait_ge(final_step, 2 * (c - 1))
                    for t in range(SPT):
                        sp.dma_start(out_steps[c - 2, t], acc[rows(t), :, :]).then_inc(stored, 16)

            macros(sp, body, loop_to=CH - 3)
            sp.wait_ge(stored, MOVES * CH)

        @block.gpsimd
        def _(pool):
            nc.gpsimd.memset(ident[:, :], 0.0).then_inc(ident_set, 1)
            nc.gpsimd.memset(spread[:, :, :], 0.0).then_inc(ident_set, 1)
            pool.wait_ge(ident_set, 2)
            nc.gpsimd.affine_select(out=ident[:, :], in_=ident[:, :], compare_op=ALU.not_equal, fill=1.0, base=0,
                                    pattern=[[-1, P]], channel_multiplier=1).then_inc(diag_set, 1)
            pool.wait_ge(diag_set, 1)
            nc.gpsimd.tensor_copy(ident_b[:, :], ident[:, :]).then_inc(ident_set, 1)
            for i in range(PARTS):
                pool.wait_ge(diag_set, i + 1)
                nc.gpsimd.affine_select(out=spread[:, :, :], in_=spread[:, :, :], compare_op=ALU.not_equal, fill=1.0,
                                        base=-i * NB, pattern=[[-1, NB], [0, N]], channel_multiplier=1).then_inc(diag_set, 1)
            pool.wait_ge(diag_set, PARTS + 1)
            pool.wait_ge(started, 1)

            def settle():
                pool.wait_ge(started, 1)

            def inverse_root(var, ve, rstd, n, mv_done, ve_done, rstd_done, q, per):
                pool.wait_ge(mv_done, per * (q + 1))
                nc.gpsimd.tensor_tensor(ve[:, :], var, eps_t[:, 0:1].broadcast_to([P, n]), ALU.add).then_inc(ve_done, 1)
                pool.wait_ge(ve_done, q + 1)
                nc.gpsimd.tensor_tensor(rstd[:, :], ve[:, :], minus_half[:, 0:1].broadcast_to([P, n]),
                                        ALU.pow).then_inc(rstd_done, 1)

            def body(c):
                prep, scan, post, ffn = (active(s, c) for s in STAGES)
                later = not isinstance(c, int)
                for k in range(T):
                    if k == 0 and ffn:
                        q = c - 2
                        pool.wait_ge(x2_step, 3 * (q + 1))
                        if later or q >= 1:
                            pool.wait_ge(final_step, 2 * q)
                        nc.gpsimd.tensor_tensor(x2_keep[:, :, :], x2[:, :, :],
                                                zero_t[:, 0:1].unsqueeze(2).broadcast_to([P, NT, D]), ALU.add).then_inc(kept, 1)
                    if k == 1 and prep:
                        q = c + 1
                        inverse_root(mv1[:, :, 1], ve1, rstd1, NT + 1, mv1_done, ve1_done, rstd1_done, q, NT + 1)
                        pool.wait_ge(xn_done, (NT + 1) * (q + 1))
                        nc.gpsimd.tensor_tensor(h[:, :, :], h[:, :, :], scale_a[:, :, :].broadcast_to([P, NT + 1, D]),
                                                ALU.mult).then_inc(h_scaled, 1)
                        pool.wait_ge(h_scaled, q + 1)
                        nc.gpsimd.tensor_tensor(h[:, :, :], h[:, :, :], shift_a[:, :, :].broadcast_to([P, NT + 1, D]),
                                                ALU.add).then_inc(h_done, 1)
                    if k == 2 and post:
                        q = c - 1
                        inverse_root(mv2[:, :, 1], ve2, rstd2, NT, mv2_done, ve2_done, rstd2_done, q, NT)
                    if k == 3:
                        if post:
                            q = c - 1
                            pool.wait_ge(on_done, NT * (q + 1))
                            nc.gpsimd.tensor_tensor(o[:, :, :], o[:, :, :], gate_g[:, :, :].broadcast_to([P, NT, D]),
                                                    ALU.mult).then_inc(x2_step, 1)
                            pool.wait_ge(x2_step, 3 * q + 1)
                            nc.gpsimd.tensor_tensor(o[:, :, :], o[:, :, :], gate_beta[:, :, :].broadcast_to([P, NT, D]),
                                                    ALU.add).then_inc(x2_step, 1)
                            pool.wait_ge(x2_step, 3 * q + 2)
                            pool.wait_ge(x_res_loaded, MOVES * (q + 1))
                            if later or q >= 1:
                                pool.wait_ge(kept, q)
                                pool.wait_ge(n2_done, NT * q)
                            nc.gpsimd.tensor_tensor(x2[:, :, :], o[:, :, :], x_res[:, :, :], ALU.add).then_inc(x2_step, 1)
                    if k == 4 and prep:
                        q = c + 1
                        pool.wait_ge(work_read, work_count("xc_next", c))
                        if later or q >= 1:
                            pool.wait_ge(xs_done, q)
                        n = (K + K) * q
                        for tap in range(K):
                            dst = cv if tap == 0 else scratch
                            if tap >= 2:
                                n_ = (n + 2 * tap - 1)
                                pool.wait_ge(conv_step, n_)
                            nc.gpsimd.tensor_tensor(dst[:, :], xc[:, tap * NB:tap * NB + TOK],
                                                    conv_w_sb[:, tap:tap + 1].broadcast_to([P, TOK]), ALU.mult)\
                              .then_inc(conv_step, 1)
                            if tap >= 1:
                                pool.wait_ge(conv_step, n + 2 * tap)
                                nc.gpsimd.tensor_tensor(cv[:, :], cv[:, :], scratch[:, :], ALU.add).then_inc(conv_step, 1)
                        pool.wait_ge(conv_step, n + 2 * K - 1)
                        nc.gpsimd.tensor_tensor(xc[:, 0:2 * NB], xc[:, TOK:TOK + 2 * NB],
                                                zero_t[:, 0:1].broadcast_to([P, 2 * NB]), ALU.add).then_inc(conv_step, 1)
                    if k == 5 and post:
                        q = c - 1
                        inverse_root(mv3[:, :, 1], ve3, rstd3, NT, mv3_done, ve3_done, rstd3_done, q, NT)
                    if k == 6 and prep:
                        q = c + 1
                        if later or q >= 2:
                            pool.wait_ge(work_read, work_count("proj", c))
                        settle()
                        nc.gpsimd.tensor_tensor(h_res[:, q % 2, :].rearrange("p (j d) -> p j d", j=NT), h[:, 0:NT, :],
                                                out_b_row[:, :, :].broadcast_to([P, NT, D]), ALU.add).then_inc(h_res_done, 1)
                    if k == 7:
                        if post:
                            q = c - 1
                            pool.wait_ge(n2_done, NT * (q + 1))
                            nc.gpsimd.tensor_tensor(h2[:, :, :], h2[:, :, :], scale_b[:, :, :].broadcast_to([P, NT, D]),
                                                    ALU.mult).then_inc(h2_step, 1)
                            pool.wait_ge(h2_step, 2 * q + 1)
                            nc.gpsimd.tensor_tensor(h2[:, :, :], h2[:, :, :], shift_b[:, :, :].broadcast_to([P, NT, D]),
                                                    ALU.add).then_inc(h2_step, 1)
                    if k == 9 and prep:
                        q = c + 1
                        pool.wait_ge(dt_done, q + 1)
                        if later or q >= 1:
                            pool.wait_ge(work_full, work_count("dtx1", c))
                        nc.gpsimd.tensor_tensor(dtx[:, :], dt[:, :], xs[:, :], ALU.mult).then_inc(dtx_done, 1)
                        n = 4 * q
                        part = [dtx_part[:, :, i, :] for i in range(PARTS)]
                        whole, rest = (v[:, :].rearrange("p (t b) -> p t b", b=NB) for v in (dtx, scratch))
                        nought = zero_t[:, 0:1].unsqueeze(2).broadcast_to([P, T, NB])
                        pool.wait_ge(dtx_done, q + 1)
                        nc.gpsimd.tensor_tensor(part[0], whole, nought, ALU.add).then_inc(parts_step, 1)
                        pool.wait_ge(parts_step, n + 1)
                        nc.gpsimd.tensor_tensor(rest, whole, part[0], ALU.subtract).then_inc(parts_step, 1)
                        pool.wait_ge(parts_step, n + 2)
                        nc.gpsimd.tensor_tensor(part[1], rest, nought, ALU.add).then_inc(parts_step, 1)
                        pool.wait_ge(parts_step, n + 3)
                        nc.gpsimd.tensor_tensor(part[2], rest, part[1], ALU.subtract).then_inc(parts_step, 1)
                    for e in range(1, EX):
                        if ffn and DOWN_AT[e] == k:
                            q = c - 2
                            pool.wait_ge(work_read, work_count(f"down{e}", c))
                            if e >= 2:
                                pool.wait_ge(acc_step, E * q + e - 1)
                            nc.gpsimd.tensor_tensor(acc[:, :, :], acc[:, :, :],
                                                    scaled[:, e % 2, :].rearrange("p (j d) -> p j d", j=NT),
                                                    ALU.add).then_inc(acc_step, 1)
                    if k == 14 and ffn:
                        q = c - 2
                        pool.wait_ge(acc_step, E * (q + 1))
                        nc.gpsimd.tensor_tensor(acc[:, :, :], acc[:, :, :], gate_b[:, :, :].broadcast_to([P, NT, D]),
                                                ALU.mult).then_inc(final_step, 1)
                        pool.wait_ge(final_step, 2 * q + 1)
                        pool.wait_ge(kept, q + 1)
                        nc.gpsimd.tensor_tensor(acc[:, :, :], acc[:, :, :], x2_keep[:, :, :],
                                                ALU.add).then_inc(final_step, 1)

            macros(pool, body)

        @block.scalar
        def _(act):
            for i, (dst, src) in enumerate(params):
                if i % 2 == 1:
                    act.dma_start(dst, src).then_inc(params_in, 16)
            act.wait_ge(params_in, 16 * len(params))
            nc.scalar.activation(cond[:, :], cond[:, :], ACT.Silu).then_inc(cond_ready, 1)
            act.wait_ge(set_up, 2)
            nc.scalar.activation(neg_a[:, :], neg_a[:, :], ACT.Exp).then_inc(a_exp, 1)
            act.wait_ge(started, 1)

            def settle():
                act.wait_ge(started, 1)

            def full(name, c):
                act.wait_ge(work_full, work_count(name, c))

            def decays(half, q, n0, n1):
                if n0 == 0:
                    act.wait_ge(dt_done, q + 1)
                    if not isinstance(q, int) or q >= 1:
                        act.wait_ge(decay_turned, T * (q - 1) + HT * (half + 1))
                for n in range(n0, n1):
                    nc.scalar.activation(decay[:, half * HT:(half + 1) * HT, :, n],
                                         dt[:, half * HT * NB:(half + 1) * HT * NB].rearrange("p (t b) -> p t b", b=NB),
                                         ACT.Exp, scale=neg_a[:, n:n + 1]).then_inc(decay_made[half], 1)

            def gelu(e, q):
                for f in range(FT):
                    act.wait_ge(up_done[f], EX * q + e + 1)
                    if f == 0 and (e >= HBUF or not isinstance(q, int) or q >= 1):
                        old = (e - HBUF, q) if e >= HBUF else (e - HBUF + EX, q - 1)
                        act.wait_ge(work_full, work_count(f"down{old[0]}", old[1] + 2))
                    nc.scalar.activation(hid[:, e % HBUF, f, :], up_ps[f][:, :], ACT.Gelu).then_inc(gelu_done[f], 1)

            def dtx_half(half):
                nc.scalar.activation(dtx_rows[:, half * HT:(half + 1) * HT, :].rearrange("p t d -> p (t d)"),
                                     work[0:PARTS * NB, :].bitcast(BF16), ACT.Copy).then_inc(work_read, 1)

            def scale_inputs(k, q):
                n = T * q + k
                act.wait_ge(input_made, n + 1)
                if not isinstance(q, int) or n >= 2:
                    act.wait_ge(added, n - 1)
                settle()
                for g in range(GV, BG):
                    last = nc.scalar.activation(scaled_in[:, k % 2, g, :], input_ps[:, g, :], ACT.Copy,
                                                scale=b_q[:, q % 2, k * BG + g:k * BG + g + 1])
                last.then_inc(scaled_a, 1)

            def body(c):
                prep, scan, post, ffn = (active(s, c) for s in STAGES)
                later = not isinstance(c, int)
                for k in range(T):
                    if k == 0 and scan:
                        full("dtx1", c)
                        if later or c >= 1:
                            act.wait_ge(input_made, T * c)
                        dtx_half(1)
                    if k == 0 and post:
                        q = c - 1
                        act.wait_ge(y_done, T * (q + 1))
                        if later or q >= 1:
                            act.wait_ge(work_full, work_count("turn_y", c - 1))
                        nc.scalar.activation(y_tok[:, :, :], y_ps[:, :, :], ACT.Copy).then_inc(y_kept, 1)
                    if ffn:
                        for e in range(EX):
                            if UP_AT[e] == k:
                                gelu(e, c - 2)
                    if k == 2:
                        if prep:
                            full("turn", c)
                            nc.scalar.activation(h_t[:, 0:TOK], work[:, :], ACT.Copy).then_inc(work_read, 1)
                            full("turn_next", c)
                            nc.scalar.activation(h_t[:, TOK:], work[:, 0:NB], ACT.Copy).then_inc(work_read, 1)
                        if scan:
                            decays(1, c, 0, 11)
                    if k == 3:
                        if prep:
                            full("xc", c)
                            if later or c >= 0:
                                act.wait_ge(conv_step, 2 * K * (c + 1))
                            nc.scalar.activation(xc[:, 2 * NB:2 * NB + TOK], work[:, :], ACT.Identity,
                                                 bias=in_b_sb[:, 0:1]).then_inc(work_read, 1)
                        if scan:
                            decays(1, c, 11, 22)
                    if k == 4 and scan:
                        decays(1, c, 22, N)
                    if k == 7 and prep:
                        q = c + 1
                        full("z", c)
                        if later or q >= 2:
                            act.wait_ge(work_read, work_count("turn_y", c))
                        settle()
                        nc.scalar.activation(z_act[:, q % 2, :], work[:, :], ACT.Silu,
                                             bias=in_b_sb[:, 1:2]).then_inc(work_read, 1)
                        act.wait_ge(conv_step, 2 * K * q + 2 * K - 1)
                        if later or q >= 1:
                            act.wait_ge(work_full, work_count("c1", c))
                            act.wait_ge(dtx_done, q)
                        nc.scalar.activation(xs[:, :], cv[:, :], ACT.Silu, bias=conv_b_sb[:, 0:1]).then_inc(xs_done, 1)
                    if k == 8 and prep:
                        q = c + 1
                        act.preload_act_table_set("natural_log_exp_and_others")
                        act.wait_ge(work_read, work_count("dt", c))
                        nc.scalar.activation(dt_raw[:, :], dt_raw[:, :], ACT.Exp).then_inc(dt_exp_done, 1)
                        act.wait_ge(dt_exp_done, q + 1)
                        nc.scalar.activation(dt_raw[:, :], dt_raw[:, :], ACT.Ln, bias=1.0).then_inc(dt_log_done, 1)
                        full("b", c)
                        settle()
                        for i in range(BQ):
                            last = nc.scalar.activation(
                                b_q[i * N:(i + 1) * N, q % 2, :],
                                work[i * N:(i + 1) * N, :].rearrange("p (g b) -> p g b", b=BQ)[:, :, i],
                                ACT.Identity, bias=b_b_col[i * N:(i + 1) * N, 0:1])
                        last.then_inc(work_read, 1)
                    if k == 9 and prep:
                        decays(0, c + 1, 0, 11)
                    if k == 10 and prep:
                        full("dtx0", c)
                        if later or c >= 0:
                            act.wait_ge(input_made, T * c + HT)
                        dtx_half(0)
                    if k == 12 and prep:
                        decays(0, c + 1, 11, 22)
                    if k == 13 and prep:
                        decays(0, c + 1, 22, N)
                    if k == 15 and post:
                        q = c - 1
                        full("turn2", c)
                        nc.scalar.activation(h2_t[:, :], work[:, :], ACT.Copy).then_inc(work_read, 1)
                        act.wait_ge(gap_done, q + 1)
                        nc.scalar.activation(rt[:, 1, :], rt[:, 0, :], ACT.Exp).then_inc(gap_exp, 1)
                    if k < T - 1 and scan:
                        scale_inputs(k + 1, c)
                    elif k == T - 1 and prep:
                        scale_inputs(0, c + 1)

            macros(act, body)

        @block.vector
        def _(dve):
            nc.vector.memset(x_in[:, NT, :], 0.0).then_inc(set_up, 1)
            dve.wait_ge(params_in, 16 * len(params))
            nc.vector.tensor_scalar(neg_a[:, :], neg_a[:, :], -5.0, 2.0, ALU.max, ALU.min).then_inc(set_up, 1)
            nc.vector.memset(edge[:, :], 1.0).then_inc(set_up, 1)
            nc.vector.memset(group_mask[:, :], 0.0).then_inc(set_up, 1)
            dve.wait_ge(set_up, 4)
            nc.vector.memset(edge[:, CH - 1:CH], 0.0).then_inc(set_up, 1)
            for i in range(BQ):
                nc.vector.memset(group_mask[i * N:(i + 1) * N, i:i + 1], 1.0).then_inc(set_up, 1)
            nc.vector.memset(eps_t[:, :], EPS).then_inc(set_up, 1)
            nc.vector.memset(minus_half[:, :], -0.5).then_inc(set_up, 1)
            nc.vector.memset(zero_t[:, :], 0.0).then_inc(set_up, 1)
            nc.vector.memset(xc[:, 0:2 * NB], 0.0).then_inc(set_up, 1)
            nc.vector.memset(state[:, 1, :], 0.0).then_inc(set_up, 1)
            nc.vector.memset(c_diag[:, :, :, :], 0.0).then_inc(set_up, 1)
            for e in range(E):
                nc.vector.memset(iota_e[:, 0, e:e + 1], float(e)).then_inc(set_up, 1)
            n = 4 + 1 + BQ + 6 + E
            dve.wait_ge(a_exp, 1)
            nc.vector.tensor_scalar(neg_a[:, :], neg_a[:, :], -1.0, None, ALU.mult).then_inc(set_up, 1)
            n += 1
            dve.wait_ge(mod_ready, 1)
            sa, ca, ga, sb_ = (up_ps[0][:, i * D:(i + 1) * D] for i in range(4))
            cb, gb = (up_ps[1][:, i * D:(i + 1) * D] for i in range(2))
            nc.vector.tensor_copy(shift_a[:, 0, :], sa).then_inc(set_up, 1)
            nc.vector.tensor_scalar(scale_a[:, 0, :], ca, 1.0, None, ALU.add).then_inc(set_up, 1)
            nc.vector.tensor_copy(shift_b[:, 0, :], sb_).then_inc(set_up, 1)
            nc.vector.tensor_scalar(scale_b[:, 0, :], cb, 1.0, None, ALU.add).then_inc(set_up, 1)
            n += 4
            for g, dst in ((ga, gate_t[:, 3, :]), (gb, gate_b[:, 0, :])):
                dve.wait_ge(set_up, n)
                nc.vector.tensor_scalar(gate_t[:, 0, :], g, -1.0, None, ALU.mult).then_inc(set_up, 1)
                nc.vector.tensor_scalar(gate_t[:, 1, :], g, 0.0, 2.0, ALU.is_ge, ALU.mult).then_inc(set_up, 1)
                dve.wait_ge(set_up, n + 2)
                nc.vector.tensor_tensor(gate_t[:, 0, :], g, gate_t[:, 0, :], ALU.max).then_inc(set_up, 1)
                nc.vector.tensor_scalar(gate_t[:, 1, :], gate_t[:, 1, :], -1.0, None, ALU.add).then_inc(set_up, 1)
                dve.wait_ge(set_up, n + 4)
                nc.vector.scalar_tensor_tensor(out=dst, in0=gate_t[:, 0, :], scalar=GATE_MIN, in1=gate_t[:, 1, :],
                                               op0=ALU.max, op1=ALU.mult).then_inc(set_up, 1)
                n += 5
            dve.wait_ge(set_up, n)
            nc.vector.tensor_tensor(gate_g[:, 0, :], gate_t[:, 3, :], g_row[:, :], ALU.mult).then_inc(set_up, 1)
            dve.wait_ge(set_up, n + 1)
            nc.vector.tensor_tensor(gate_beta[:, 0, :], gate_t[:, 3, :], beta_row[:, :], ALU.mult).then_inc(started, 1)

            def settle():
                dve.wait_ge(started, 1)

            def moments(src, bn, mv, tiles, mv_done):
                for j in range(tiles):
                    nc.vector.bn_stats(bn[:, j, :], src[:, j, :])
                nc.vector.drain()
                for j in range(tiles):
                    nc.vector.bn_aggr(mv[:, j, :], bn[:, j, :]).then_inc(mv_done, 1)

            def normalise(dst, src, mv, rstd, tiles, done):
                for j in range(tiles):
                    nc.vector.tensor_scalar(dst[:, j, :], src[:, j, :], mv[:, j, 0:1], rstd[:, j:j + 1],
                                            ALU.subtract, ALU.mult).then_inc(done, 1)

            def full(name, c):
                dve.wait_ge(work_full, work_count(name, c))

            def c_diagonal(half):
                nc.vector.scalar_tensor_tensor(
                    out=c_diag[:, half * HT:(half + 1) * HT, :, 0:BQ].rearrange("p t g b -> p (t g) b"),
                    in0=work[:, 0:TOK // 2].rearrange("p (g b) -> p g b", b=BQ), scalar=c_b_col[:, 0:1],
                    in1=group_mask[:, :].unsqueeze(1).broadcast_to([P, HT * BG, BQ]),
                    op0=ALU.add, op1=ALU.mult).then_inc(work_read, 1)

            def scan_step(k, c):
                n = T * c + k
                dve.wait_ge(input_made, n + 1)
                nc.vector.tensor_tensor(scaled_in[:, k % 2, 0:GV, :], input_ps[:, 0:GV, :],
                                        b_q[:, c % 2, k * BG:k * BG + GV].unsqueeze(2).broadcast_to([P, GV, D]),
                                        ALU.mult).then_inc(scaled_v, 1)
                dve.wait_ge(decay_turned, n + 1)
                if not isinstance(c, int) or n >= 1:
                    dve.wait_ge(state_done, n)
                nc.vector.tensor_tensor(prod[:, :], decay_ps[:, :, :].rearrange("p g d -> p (g d)"),
                                        state[:, (k + 1) % 2, :], ALU.mult).then_inc(decayed, 1)
                dve.wait_ge(scaled_v, n + 1)
                dve.wait_ge(scaled_a, n + 1)
                dve.wait_ge(decayed, n + 1)
                nc.vector.tensor_tensor(prod[:, :], scaled_in[:, k % 2, :, :].rearrange("p g d -> p (g d)"), prod[:, :],
                                        ALU.add).then_inc(added, 1)
                dve.wait_ge(added, n + 1)
                if not isinstance(c, int) or n >= 2:
                    dve.wait_ge(y_done, n - 1)
                nc.vector.tensor_scalar(state[:, k % 2, :], prod[:, :], -CLIP, CLIP, ALU.max,
                                        ALU.min).then_inc(state_done, 1)

            def body(c):
                prep, scan, post, ffn = (active(s, c) for s in STAGES)
                later = not isinstance(c, int)
                for k in range(T):
                    if scan:
                        scan_step(k, c)
                    if k == 0:
                        if scan:
                            full("c1", c)
                            if later or c >= 1:
                                dve.wait_ge(y_done, T * c)
                            c_diagonal(1)
                        if post:
                            q = c - 1
                            full("turn_y", c)
                            settle()
                            nc.vector.tensor_tensor(yz[:, :], work[:, :], z_act[:, q % 2, :], ALU.mult).then_inc(work_read, 1)
                        if prep:
                            q = c + 1
                            dve.wait_ge(x_loaded, LOADS * (q + 1))
                            moments(x_in, bn1, mv1, NT + 1, mv1_done)
                    if k == 1:
                        if post:
                            q = c - 1
                            full("proj", c)
                            dve.wait_ge(h_res_done, q + 1)
                            if later or q >= 1:
                                dve.wait_ge(x2_step, 3 * q)
                            settle()
                            nc.vector.tensor_tensor(o[:, :, :].rearrange("p j d -> p (j d)"), work[:, :],
                                                    h_res[:, q % 2, :], ALU.add).then_inc(work_read, 1)
                        if prep:
                            q = c + 1
                            dve.wait_ge(rstd1_done, q + 1)
                            if later or q >= 1:
                                dve.wait_ge(work_full, work_count("turn_next", c - 1))
                                dve.wait_ge(h_res_done, q)
                            normalise(h, x_in, mv1, rstd1, NT + 1, xn_done)
                        if post:
                            dve.wait_ge(work_read, work_count("proj", c))
                            moments(o, bn2, mv2, NT, mv2_done)
                    if k == 2 and post:
                        q = c - 1
                        dve.wait_ge(rstd2_done, q + 1)
                        normalise(o, o, mv2, rstd2, NT, on_done)
                    if k == 4:
                        if prep:
                            q = c + 1
                            full("xc_next", c)
                            if later or q >= 1:
                                dve.wait_ge(conv_step, 2 * K * q)
                            nc.vector.tensor_scalar(xc[:, 2 * NB + TOK:], work[:, 0:NB], in_b_sb[:, 0:1],
                                                    edge[:, q:q + 1] if isinstance(q, int) else edge_col(q), ALU.add, ALU.mult)\
                              .then_inc(work_read, 1)
                        if post:
                            q = c - 1
                            dve.wait_ge(x2_step, 3 * (q + 1))
                            moments(x2, bn3, mv3, NT, mv3_done)
                    if k == 6 and post:
                        q = c - 1
                        dve.wait_ge(rstd3_done, q + 1)
                        if later or q >= 1:
                            dve.wait_ge(work_full, work_count("turn2", c - 1))
                        normalise(h2, x2, mv3, rstd3, NT, n2_done)
                    if k == 8 and prep:
                        q = c + 1
                        full("dt", c)
                        if later or q >= 1:
                            dve.wait_ge(dt_done, q)
                        nc.vector.tensor_scalar(dt_raw[:, :], work[:, :], dt_b_sb[:, 0:1], DT_IN_MAX, ALU.add,
                                                ALU.min).then_inc(work_read, 1)
                    if k == 9 and prep:
                        q = c + 1
                        dve.wait_ge(dt_log_done, q + 1)
                        if later or q >= 1:
                            dve.wait_ge(decay_made[1], N * q)
                            dve.wait_ge(dtx_done, q)
                        nc.vector.tensor_scalar(dt[:, :], dt_raw[:, :], DT_MIN, DT_MAX, ALU.max, ALU.min).then_inc(dt_done, 1)
                        full("c0", c)
                        if later or q >= 1:
                            dve.wait_ge(y_done, T * c + HT)
                        c_diagonal(0)
                    if ffn:
                        for e in range(EX):
                            if DOWN_AT[e] == k:
                                q = c - 2
                                full(f"down{e}", c)
                                if e == 0:
                                    if later or q >= 1:
                                        dve.wait_ge(stored, MOVES * q)
                                    nc.vector.tensor_copy(acc[:, :, :], work[:, :].rearrange("p (j d) -> p j d", d=D))\
                                      .then_inc(work_read, 1)
                                else:
                                    if e >= 3:
                                        dve.wait_ge(acc_step, E * q + e - 2)
                                    nc.vector.tensor_tensor(
                                        scaled[:, e % 2, :].rearrange("p (j d) -> p j d", d=D),
                                        work[:, :].rearrange("p (j d) -> p j d", d=D),
                                        cw[:, :, e - 1:e].broadcast_to([P, NT, D]), ALU.mult).then_inc(work_read, 1)
                    if k == 15 and post:
                        route(c, c - 1)

            def edge_col(q):
                return edge[:, :].rearrange("p (c o) -> p c o", o=1)[:, q, :]

            def route(c, q):
                full("logits", c)
                nc.vector.tensor_copy(lg[:, :, :], work[:, 0:NT * E].rearrange("p (j e) -> p j e", e=E)).then_inc(work_read, 1)
                nc.vector.drain()
                for j in range(NT):
                    nc.vector.max(top_v[:, j, :], lg[:, j, :])
                nc.vector.drain()
                for j in range(NT):
                    nc.vector.max_index(top_i[:, j, :], top_v[:, j, :], lg[:, j, :]).then_inc(index_done, 1)
                nc.vector.tensor_tensor(rt[:, 0, :], top_v[:, :, 1], top_v[:, :, 0], ALU.subtract).then_inc(gap_done, 1)
                dve.wait_ge(index_done, NT * (q + 1))
                nc.vector.tensor_copy(top_f[:, :, :], top_i[:, :, 0:2]).then_inc(route_step, 1)
                dve.wait_ge(gap_exp, q + 1)
                n = 9 * q
                nc.vector.tensor_scalar(rt[:, 2, :], rt[:, 1, :], 1.0, None, ALU.add).then_inc(route_step, 1)
                dve.wait_ge(route_step, n + 2)
                nc.vector.reciprocal(rt[:, 3, :], rt[:, 2, :]).then_inc(route_step, 1)
                dve.wait_ge(route_step, n + 3)
                nc.vector.tensor_tensor(rt[:, 2, :], rt[:, 1, :], rt[:, 3, :], ALU.mult).then_inc(route_step, 1)
                for i in range(2):
                    nc.vector.tensor_tensor(pick[:, i, :, :], iota_e[:, :, :].broadcast_to([P, NT, E]),
                                            top_f[:, :, i:i + 1].broadcast_to([P, NT, E]), ALU.is_equal).then_inc(route_step, 1)
                dve.wait_ge(route_step, n + 6)
                for i, share in enumerate((3, 2)):
                    nc.vector.tensor_tensor(pick[:, i, :, :], pick[:, i, :, :],
                                            rt[:, share, :].unsqueeze(2).broadcast_to([P, NT, E]), ALU.mult).then_inc(route_step, 1)
                dve.wait_ge(route_step, n + 8)
                nc.vector.tensor_tensor(cw[:, :, :], pick[:, 0, :, :], pick[:, 1, :, :], ALU.add).then_inc(route_step, 1)

            macros(dve, body)

        @block.tensor
        def _(pe):
            pe.wait_ge(cond_ready, 1)
            nc.tensor.matmul(up_ps[0][:, :], cond[:, :], wmod_sb[:, 0:4 * D], start=True, stop=True)
            nc.tensor.matmul(up_ps[1][:, 0:2 * D], cond[:, :], wmod_sb[:, 4 * D:], start=True, stop=True).then_inc(mod_ready, 1)
            pe.wait_ge(started, 1)
            pe.wait_ge(diag_set, 1)
            pe.wait_ge(ident_set, 3)

            def free_work(name, c):
                count = work_count(name, c) - 1
                if not isinstance(c, int) or count >= 1:
                    pe.wait_ge(work_read, count)

            def turn_decays(k, q):
                n = T * q + k
                if k % HT == 0:
                    pe.wait_ge(decay_made[k // HT], N * (q + 1))
                if not isinstance(q, int) or n >= 1:
                    pe.wait_ge(decayed, n)
                for g in range(BG):
                    last = nc.tensor.transpose(decay_ps[:, g, :],
                                               decay[:, k, g * BQ:(g + 1) * BQ, :].rearrange("p b n -> p (b n)"), ident[:, :])
                last.then_inc(decay_turned, 1)

            def make_inputs(k, q):
                n = T * q + k
                if k == 0:
                    pe.wait_ge(work_read, work_count("dtx0", q - 1))
                if k == HT:
                    pe.wait_ge(work_read, work_count("dtx1", q))
                if not isinstance(q, int) or n >= 1:
                    pe.wait_ge(scaled_v, n)
                    pe.wait_ge(scaled_a, n)
                for g in range(BG):
                    last = nc.tensor.matmul(input_ps[:, g, :],
                                            spread[:, g * BQ:(g + 1) * BQ, :].rearrange("p b n -> p (b n)"),
                                            dtx_rows[:, k, :], start=True, stop=True)
                last.then_inc(input_made, 1)

            def read_out(k, q):
                n = T * q + k
                pe.wait_ge(state_done, n + 1)
                if k == 0:
                    pe.wait_ge(work_read, work_count("c0", q - 1))
                    if not isinstance(q, int) or q >= 1:
                        pe.wait_ge(y_kept, q)
                if k == HT:
                    pe.wait_ge(work_read, work_count("c1", q))
                blocks = c_diag[:, k, :, :].rearrange("p g b -> p (g b)")
                for g in range(BG):
                    last = nc.tensor.matmul(y_ps[rows(k % SPT), k // SPT, :], blocks[:, g * NB:(g + 1) * NB],
                                            state[:, k % 2, g * D:(g + 1) * D], start=(g == 0), stop=(g == BG - 1))
                last.then_inc(y_done, 1)

            def turn(src, tiles):
                for i, j in enumerate(tiles):
                    last = nc.tensor.transpose(work[:, i * P:(i + 1) * P], src(j), ident[:, :])
                return last

            def use(name, c):
                free_work(name, c)
                if name in ("dtx0", "dtx1"):
                    q = c + 1 if name == "dtx0" else c
                    pe.wait_ge(parts_step, 4 * (q + 1))
                    pe.wait_ge(diag_set, PARTS + 1)
                    for t in range(HT):
                        last = nc.tensor.transpose(
                            work[0:PARTS * NB, :].bitcast(BF16)[:, t * D:(t + 1) * D],
                            dtx_part[:, int(name[-1]) * HT + t, :, :].rearrange("p i b -> p (i b)"), ident_b[:, :])
                elif name in ("c0", "c1"):
                    q = c + 1 if name == "c0" else c
                    pe.wait_ge(xs_done, q + 1)
                    half = int(name[-1]) * TOK // 2
                    last = nc.tensor.matmul(work[:, 0:TOK // 2], c_w_sb[:, :], xs[:, half:half + TOK // 2], start=True, stop=True)
                elif name == "turn":
                    pe.wait_ge(h_done, c + 2)
                    last = turn(lambda j: h[:, j, :], range(NT))
                elif name == "turn_next":
                    last = turn(lambda j: h[:, j, :], [NT])
                elif name == "xc":
                    last = nc.tensor.matmul(work[:, :], in_w_sb[:, 0:D], h_t[:, 0:TOK], start=True, stop=True)
                elif name == "xc_next":
                    last = nc.tensor.matmul(work[:, 0:NB], in_w_sb[:, 0:D], h_t[:, TOK:], start=True, stop=True)
                elif name == "z":
                    last = nc.tensor.matmul(work[:, :], in_w_sb[:, D:], h_t[:, 0:TOK], start=True, stop=True)
                elif name == "dt":
                    pe.wait_ge(xs_done, c + 2)
                    last = nc.tensor.matmul(work[:, :], dt_w_sb[:, :], xs[:, :], start=True, stop=True)
                elif name == "b":
                    last = nc.tensor.matmul(work[:, :], b_w_sb[:, :], xs[:, :], start=True, stop=True)
                elif name == "turn_y":
                    pe.wait_ge(y_kept, c)
                    last = turn(lambda j: y_tok[:, j, :], range(NT))
                elif name == "proj":
                    for j in range(NT):
                        last = nc.tensor.matmul(work[:, j * D:(j + 1) * D], yz[:, j * P:(j + 1) * P], out_w_sb[:, :],
                                                start=True, stop=True)
                elif name == "turn2":
                    pe.wait_ge(h2_step, 2 * c)
                    last = turn(lambda j: h2[:, j, :], range(NT))
                elif name == "logits":
                    for j in range(NT):
                        last = nc.tensor.matmul(work[:, j * E:(j + 1) * E], h2_t[:, j * P:(j + 1) * P], wg_sb[:, :],
                                                start=True, stop=True)
                else:
                    e = int(name[4:])
                    for f in range(FT):
                        pe.wait_ge(gelu_done[f], EX * (c - 2) + e + 1)
                    for j in range(NT):
                        for f in range(FT):
                            last = nc.tensor.matmul(work[:, j * D:(j + 1) * D], hid[:, e % HBUF, f, j * P:(j + 1) * P],
                                                    wd_sb[:, e, f, :], start=(f == 0), stop=(f == FT - 1))
                last.then_inc(work_full, 1)

            def uses(k, place, c):
                for where, stage, name in at_step(k):
                    if where == place and active(stage, c):
                        use(name, c)

            def up(e, q):
                for f in range(FT):
                    if e >= 1 or not isinstance(q, int) or q >= 1:
                        pe.wait_ge(gelu_done[f], EX * q + e)
                    nc.tensor.matmul(up_ps[f][:, :], wu_sb[:, e, f * P:(f + 1) * P], h2_t[:, :], start=True, stop=True)\
                      .then_inc(up_done[f], 1)

            def body(c):
                prep, scan, post, ffn = (active(s, c) for s in STAGES)
                for k in range(T):
                    uses(k, "a", c)
                    if k > 0 and scan:
                        read_out(k - 1, c)
                    elif k == 0 and active("scan", c - 1 if isinstance(c, int) else c):
                        read_out(T - 1, c - 1)
                    if ffn:
                        if k == 0:
                            if isinstance(c, int) and c == 2:
                                pe.wait_ge(ffn_in, 32)
                            pe.wait_ge(work_read, work_count("turn2", c - 1))
                        for e in range(EX):
                            if UP_AT[e] == k and (e == 0 or UP_AT[e - 1] != k):
                                up(e, c - 2)
                    uses(k, "b", c)
                    if k < T - 1 and scan:
                        turn_decays(k + 1, c)
                        make_inputs(k + 1, c)
                    elif k == T - 1 and prep:
                        turn_decays(0, c + 1)
                        make_inputs(0, c + 1)
                    if ffn:
                        for e in range(1, EX):
                            if UP_AT[e] == k and UP_AT[e - 1] == k:
                                up(e, c - 2)
                    uses(k, "c", c)

            macros(pe, body)


_INS = ["x", "in_w", "in_b", "conv_w", "conv_b", "a_log", "b_w", "b_b", "c_w", "c_b", "dt_w", "dt_b", "out_w",
        "out_b", "ln_g", "ln_beta", "wg", "wu", "wd", "c_t", "wmod"]


def kernel(**inputs):
    import concourse.bacc as _bacc
    from concourse.bass_utils import run_bass_kernel_spmd as _run

    g = {name[3:]: np.asarray(a) for name, a in inputs.items()}

    def rows_of(v):
        return np.broadcast_to(v, (P, v.shape[0]))

    laid = {
        "x": g["attn_x"],
        "in_w": g["attn_in_proj_w"].T,
        "in_b": g["attn_in_proj_b"].reshape(2, D).T,
        "conv_w": g["attn_conv_w"].reshape(D, K),
        "conv_b": g["attn_conv_b"].reshape(D, 1),
        "a_log": g["attn_A_log"],
        "b_w": np.tile(g["attn_B_w"].T, (1, BQ)),
        "b_b": np.tile(g["attn_B_b"], BQ).reshape(P, 1),
        "c_w": np.tile(g["attn_C_w"].T, (1, BQ)),
        "c_b": np.tile(g["attn_C_b"], BQ).reshape(P, 1),
        "dt_w": g["attn_dt_w"].T,
        "dt_b": g["attn_dt_b"].reshape(D, 1),
        "out_w": g["attn_out_w"].T,
        "out_b": rows_of(g["attn_out_b"]),
        "ln_g": rows_of(g["attn_ln_g"]),
        "ln_beta": rows_of(g["attn_ln_beta"]),
        "wg": g["ffn_Wg"],
        "wu": np.concatenate([g["ffn_W1"][None], g["ffn_Wu"]]).transpose(1, 0, 2),
        "wd": np.concatenate([g["ffn_W2"][None], g["ffn_Wd"]]).reshape(EX, FT, P, D).transpose(2, 0, 1, 3),
        "c_t": np.tile(g["c"].T, (1, SPT)),
        "wmod": g["wmod"],
    }
    nc = _bacc.Bacc("TRN2", target_bir_lowering=False, num_devices=1)
    arrays, args = {}, []
    for name in _INS:
        a = np.ascontiguousarray(laid[name])
        arrays[f"in_{name}"] = a
        args.append(nc.dram_tensor(f"in_{name}", a.shape, mybir.dt.from_np(a.dtype), kind="ExternalInput").ap())
    args.append(nc.dram_tensor("out_y", (NB, L, D), F32, kind="ExternalOutput").ap())
    adaln_block(nc, *args)
    r = _run(nc, [arrays], core_ids=[0])
    return r.results[0]["out_y"]
```

```python
from contextlib import ExitStack

import numpy as np

import concourse.bass as bass
from concourse import mybir

F32 = mybir.dt.float32
BF16 = mybir.dt.bfloat16
U32 = mybir.dt.uint32
ALU = mybir.AluOpType
ACT = mybir.ActivationFunctionType

NB, L, D, N, K = 32, 256, 128, 32, 4
F, E, MOD = 256, 8, 6
P = 128
T = 16
TOK = T * NB
NT = TOK // P
SPT = P // NB
CH = L // T
BQ = P // N
BG = NB // BQ
HT = T // 2
FT = F // P
EX = E + 1
PARTS = 3
GV = 4
HBUF = 3
CLIP, EPS = 10.0, 1e-5
DT_MIN, DT_MAX, DT_IN_MAX = 0.001, 0.2, 20.0
GATE_MIN = 0.25

UP_AT = (1, 2, 3, 6, 7, 8, 11, 12, 13)

DECAYS_AT = [(15, 1, 1, 0, 9), (0, 1, 0, 9, 17), (1, 1, 0, 17, 19), (5, 1, 0, 19, 26), (6, 1, 0, 26, N),
             (8, 0, 1, 0, 7), (9, 0, 1, 7, 17), (10, 0, 1, 17, 28), (11, 0, 1, 28, N)]
EXP_TABLE_AT = (5, 8, 15)

WORK = [
    (0, "a", "prep", "xc"),
    (1, "a", "prep", "turn_next"),
    (2, "a", "prep", "xc_next"), (2, "b", "scan", "dtx1"),
    (3, "a", "post", "turn_y"), (3, "b", "scan", "c1"),
    (4, "a", "prep", "z"), (4, "b", "prep", "dt"),
    (5, "b", "ffn", "down0"),
    (6, "a", "post", "proj"), (6, "b", "ffn", "down1"),
    (7, "a", "prep", "b"), (7, "b", "ffn", "down2"),
    (8, "b", "ffn", "down3"), (9, "b", "ffn", "down4"), (10, "b", "ffn", "down5"),
    (11, "a", "prep", "c0"), (12, "a", "prep", "dtx0"), (12, "b", "ffn", "down6"),
    (13, "b", "ffn", "down7"), (14, "a", "post", "turn2"), (14, "b", "ffn", "down8"),
    (15, "a", "post", "logits"), (15, "b", "norm", "turn"),
]
STAGES = ("norm", "prep", "scan", "post", "ffn")
LAG = {"norm": -2, "prep": -1, "scan": 0, "post": 1, "ffn": 2}
USES = {s: sum(u[2] == s for u in WORK) for s in STAGES}
FULL_FROM, FULL_TO = 2, CH - 2
LOOP_FROM, LOOP_TO = FULL_FROM + 1, FULL_TO


def read_at(e):
    k, place = next((u[0], u[1]) for u in WORK if u[3] == f"down{e}")
    return (k, False) if place == "a" else (k + 1, True)


def active(stage, c):
    return not isinstance(c, int) or 0 <= c - LAG[stage] < CH


def work_before(c):
    if isinstance(c, int):
        return sum(USES[s] * min(max(c - LAG[s], 0), CH) for s in STAGES)
    return c * sum(USES.values()) - sum(USES[s] * LAG[s] for s in STAGES)


def work_count(name, c):
    n = 0
    for _, _, stage, use in WORK:
        n += active(stage, c)
        if use == name:
            return work_before(c) + n
    raise KeyError(name)


def macros(eng, body, loop_to=LOOP_TO):
    for c in range(-2, LOOP_FROM):
        body(c)
    with eng.Fori(LOOP_FROM, loop_to) as c:
        body(c)
    for c in range(loop_to, CH + 2):
        body(c)


def adaln_block(nc, x, in_w, in_b, conv_w, conv_b, a_log, b_w, b_b, c_w, c_b, dt_w, dt_b, out_w, out_b,
                ln_g, ln_beta, wg, wu, wd, c_t, wmod, out):
    ctx = ExitStack()
    with ctx:
        def sb(name, shape, dt=F32):
            return ctx.enter_context(nc.sbuf_tensor(name, shape, dt))

        def ps(name, shape):
            return ctx.enter_context(nc.psum_tensor(name, shape, F32))

        def sem(name):
            return ctx.enter_context(nc.semaphore(name))

        in_w_sb = sb("in_w_sb", [P, 2 * D])
        dt_w_sb = sb("dt_w_sb", [P, D])
        b_w_sb = sb("b_w_sb", [P, BQ * N])
        c_w_sb = sb("c_w_sb", [P, BQ * N])
        out_w_sb = sb("out_w_sb", [P, D])
        wg_sb = sb("wg_sb", [P, E])
        wu_sb = sb("wu_sb", [P, EX, F])
        wd_sb = sb("wd_sb", [P, EX, FT, D])
        cond = sb("cond", [P, P])
        in_b_sb = sb("in_b_sb", [P, 2])
        conv_w_sb = sb("conv_w_sb", [P, K])
        conv_b_sb = sb("conv_b_sb", [P, 1])
        neg_a = sb("neg_a", [P, N])
        b_b_col = sb("b_b_col", [P, 1])
        c_b_col = sb("c_b_col", [P, 1])
        dt_b_sb = sb("dt_b_sb", [P, 1])
        out_b_row = sb("out_b_row", [P, 1, D])
        g_row = sb("g_row", [P, D])
        beta_row = sb("beta_row", [P, D])
        ident = sb("ident", [P, P])
        shift_a = sb("shift_a", [P, 1, D])
        scale_a = sb("scale_a", [P, 1, D])
        gate_g = sb("gate_g", [P, 1, D])
        gate_beta = sb("gate_beta", [P, 1, D])
        shift_b = sb("shift_b", [P, 1, D])
        scale_b = sb("scale_b", [P, 1, D])
        gate_b = sb("gate_b", [P, 1, D])
        spread = sb("spread", [PARTS * NB, NB, N], BF16)
        group_mask = sb("group_mask", [P, BQ])
        ident_b = sb("ident_b", [P, P], BF16)
        edge = sb("edge", [P, 1, CH])
        eps_t = sb("eps_t", [P, 1])
        minus_half = sb("minus_half", [P, 1])
        zero_t = sb("zero_t", [P, 1])
        iota_e = sb("iota_e", [P, 1, E])

        x_in = sb("x_in", [P, NT + 1, D])
        bn1 = sb("bn1", [P, NT + 1, 6])
        mv1 = sb("mv1", [P, NT + 1, 2])
        ve1 = sb("ve1", [P, NT + 1])
        rstd1 = sb("rstd1", [P, NT + 1])
        h = sb("h", [P, NT + 1, D])
        h_res = sb("h_res", [P, 2, TOK])
        h_t = sb("h_t", [P, TOK + NB])
        xc = sb("xc", [P, (T + K - 1) * NB])
        cv = sb("cv", [P, TOK])
        xs = sb("xs", [P, TOK])
        z_act = sb("z_act", [P, 2, TOK])
        dt_raw = sb("dt_raw", [P, TOK])
        dt = sb("dt", [P, TOK])
        dtx = sb("dtx", [P, TOK])
        scratch = sb("scratch", [P, TOK])
        dtx_part = sb("dtx_part", [P, T, PARTS, NB], BF16)
        dtx_rows = sb("dtx_rows", [PARTS * NB, T, D], BF16)
        b_q = sb("b_q", [P, 2, T * BG])
        c_diag = sb("c_diag", [P, T, BG, NB + BQ])
        decay = sb("decay", [P, T, NB, N])
        state = sb("state", [P, 2, BG * D])
        scaled_in = sb("scaled_in", [P, 2, BG, D])
        prod = sb("prod", [P, BG * D])
        y_tok = sb("y_tok", [P, NT, D])
        yz = sb("yz", [P, TOK])
        o = sb("o", [P, NT, D])
        bn2 = sb("bn2", [P, NT, 6])
        mv2 = sb("mv2", [P, NT, 2])
        ve2 = sb("ve2", [P, NT])
        rstd2 = sb("rstd2", [P, NT])
        x_res = sb("x_res", [P, NT, D])
        x2 = sb("x2", [P, NT, D])
        bn3 = sb("bn3", [P, NT, 6])
        mv3 = sb("mv3", [P, NT, 2])
        ve3 = sb("ve3", [P, NT])
        rstd3 = sb("rstd3", [P, NT])
        h2 = sb("h2", [P, NT, D])
        h2_t = sb("h2_t", [P, TOK])
        lg = sb("lg", [P, NT, E])
        top_v = sb("top_v", [P, NT, 8])
        top_i = sb("top_i", [P, NT, 8], U32)
        top_f = sb("top_f", [P, NT, 2])
        rt = sb("rt", [P, 4, NT])
        pick = sb("pick", [P, 2, NT, E])
        cw = sb("cw", [P, NT, E])
        hid = sb("hid", [P, HBUF, FT, TOK])
        wmod_sb = hid[:, 0, :, :].rearrange("p f t -> p (f t)")[:, 0:MOD * D]
        gate_t = hid[:, 1, 0, :].rearrange("p (i d) -> p i d", i=4)
        scaled = sb("scaled", [P, 2, TOK])
        acc = sb("acc", [P, NT, D])
        x2_keep = sb("x2_keep", [P, NT, D])

        decay_ps = ps("decay_ps", [P, BG, D])
        input_ps = ps("input_ps", [P, BG, D])
        y_ps = ps("y_ps", [P, NT, D])
        up_ps = [ps(f"up_ps{f}", [P, TOK]) for f in range(FT)]
        work = ps("work", [P, TOK])

        params_in = sem("params_in")
        ffn_in = sem("ffn_in")
        ident_set = sem("ident_set")
        diag_set = sem("diag_set")
        consts_set = sem("consts_set")
        cond_ready = sem("cond_ready")
        mod_ready = sem("mod_ready")
        set_up = sem("set_up")
        a_exp = sem("a_exp")
        started = sem("started")
        diag_clear = sem("diag_clear")
        work_full = sem("work_full")
        work_read = sem("work_read")
        x_loaded = sem("x_loaded")
        mv1_done = sem("mv1_done")
        ve1_done = sem("ve1_done")
        rstd1_done = sem("rstd1_done")
        xn_done = sem("xn_done")
        h_scaled = sem("h_scaled")
        h_done = sem("h_done")
        h_res_done = sem("h_res_done")
        conv_step = sem("conv_step")
        xs_done = sem("xs_done")
        dt_exp_done = sem("dt_exp_done")
        dt_log_done = sem("dt_log_done")
        dt_done = sem("dt_done")
        dtx_done = sem("dtx_done")
        parts_step = sem("parts_step")
        decay_made = [sem("decay_made0"), sem("decay_made1")]
        decay_turned = sem("decay_turned")
        input_made = sem("input_made")
        scaled_v = sem("scaled_v")
        scaled_a = sem("scaled_a")
        decayed = sem("decayed")
        added = sem("added")
        state_done = sem("state_done")
        y_done = sem("y_done")
        y_kept = sem("y_kept")
        x_res_loaded = sem("x_res_loaded")
        mv2_done = sem("mv2_done")
        ve2_done = sem("ve2_done")
        rstd2_done = sem("rstd2_done")
        on_done = sem("on_done")
        x2_step = sem("x2_step")
        mv3_done = sem("mv3_done")
        ve3_done = sem("ve3_done")
        rstd3_done = sem("rstd3_done")
        n2_done = sem("n2_done")
        h2_step = sem("h2_step")
        index_done = sem("index_done")
        gap_done = sem("gap_done")
        gap_exp = sem("gap_exp")
        route_step = sem("route_step")
        up_done = [sem(f"up_done{f}") for f in range(FT)]
        gelu_done = [sem(f"gelu_done{f}") for f in range(FT)]
        acc_step = sem("acc_step")
        kept = sem("kept")
        final_step = sem("final_step")
        stored = sem("stored")

        block = ctx.enter_context(nc.Block())

        params = [(in_w_sb[:, :], in_w), (in_b_sb[:, :], in_b), (conv_w_sb[:, :], conv_w), (conv_b_sb[:, :], conv_b),
                  (neg_a[:, :], a_log), (b_w_sb[:, :], b_w), (b_b_col[:, :], b_b), (c_w_sb[:, :], c_w),
                  (c_b_col[:, :], c_b), (dt_w_sb[:, :], dt_w), (dt_b_sb[:, :], dt_b), (out_w_sb[:, :], out_w),
                  (out_b_row[:, 0, :], out_b), (g_row[:, :], ln_g), (beta_row[:, :], ln_beta), (wg_sb[:, :], wg),
                  (cond[:, :], c_t), (wmod_sb[:, :], wmod)]
        x_steps = x.rearrange("b (c j t) d -> c t b j d", c=CH, t=SPT)
        out_steps = out.rearrange("b (c j t) d -> c t b j d", c=CH, t=SPT)
        LOADS = 16 * (SPT + 1)
        MOVES = 16 * SPT

        def rows(t):
            return slice(t * NB, (t + 1) * NB)

        def at_step(k):
            return [u[1:] for u in WORK if u[0] == k]

        @block.sync
        def _(sp):
            def load_x(q):
                for t in range(SPT):
                    sp.dma_start(x_in[rows(t), 0:NT, :], x_steps[q, t]).then_inc(x_loaded, 16)
                ahead = min(q + 1, CH - 1) if isinstance(q, int) else q + 1
                sp.dma_start(x_in[rows(0), NT, :], x_steps[ahead, 0][:, 0, :]).then_inc(x_loaded, 16)

            for i, (dst, src) in enumerate(params):
                if i % 2 == 0:
                    sp.dma_start(dst, src).then_inc(params_in, 16)
            sp.wait_ge(set_up, 1)
            load_x(0)
            sp.dma_start(wu_sb[:, :, :], wu).then_inc(ffn_in, 16)
            sp.dma_start(wd_sb[:, :, :, :], wd).then_inc(ffn_in, 16)

            def body(c):
                if active("scan", c):
                    if not isinstance(c, int) or c >= 1:
                        sp.wait_ge(x2_step, 3 * c)
                    for t in range(SPT):
                        sp.dma_start(x_res[rows(t), :, :], x_steps[c, t]).then_inc(x_res_loaded, 16)
                if not isinstance(c, int) or 0 < c + 3 < CH:
                    sp.wait_ge(xn_done, (NT + 1) * (c + 3))
                    load_x(c + 3)
                if active("ffn", c):
                    sp.wait_ge(final_step, 2 * (c - 1))
                    for t in range(SPT):
                        sp.dma_start(out_steps[c - 2, t], acc[rows(t), :, :]).then_inc(stored, 16)

            macros(sp, body, loop_to=CH - 4)
            sp.wait_ge(stored, MOVES * CH)

        @block.gpsimd
        def _(pool):
            nc.gpsimd.memset(ident[:, :], 0.0).then_inc(ident_set, 1)
            nc.gpsimd.memset(spread[:, :, :], 0.0).then_inc(ident_set, 1)
            pool.wait_ge(ident_set, 2)
            nc.gpsimd.affine_select(out=ident[:, :], in_=ident[:, :], compare_op=ALU.not_equal, fill=1.0, base=0,
                                    pattern=[[-1, P]], channel_multiplier=1).then_inc(diag_set, 1)
            pool.wait_ge(diag_set, 1)
            nc.gpsimd.tensor_copy(ident_b[:, :], ident[:, :]).then_inc(ident_set, 1)
            for i in range(PARTS):
                pool.wait_ge(diag_set, i + 1)
                nc.gpsimd.affine_select(out=spread[:, :, :], in_=spread[:, :, :], compare_op=ALU.not_equal, fill=1.0,
                                        base=-i * NB, pattern=[[-1, NB], [0, N]], channel_multiplier=1).then_inc(diag_set, 1)
            pool.wait_ge(diag_set, PARTS + 1)
            pool.wait_ge(started, 1)

            def settle():
                pool.wait_ge(started, 1)

            def inverse_root(var, ve, rstd, n, mv_done, ve_done, rstd_done, q, per):
                pool.wait_ge(mv_done, per * (q + 1))
                nc.gpsimd.tensor_tensor(ve[:, :], var, eps_t[:, 0:1].broadcast_to([P, n]), ALU.add).then_inc(ve_done, 1)
                pool.wait_ge(ve_done, q + 1)
                nc.gpsimd.tensor_tensor(rstd[:, :], ve[:, :], minus_half[:, 0:1].broadcast_to([P, n]),
                                        ALU.pow).then_inc(rstd_done, 1)

            def body(c):
                norm, prep, scan, post, ffn = (active(s, c) for s in STAGES)
                later = not isinstance(c, int)
                for k in range(T):
                    if k == 0 and ffn:
                        q = c - 2
                        pool.wait_ge(x2_step, 3 * (q + 1))
                        if later or q >= 1:
                            pool.wait_ge(final_step, 2 * q)
                        nc.gpsimd.tensor_tensor(x2_keep[:, :, :], x2[:, :, :],
                                                zero_t[:, 0:1].unsqueeze(2).broadcast_to([P, NT, D]), ALU.add).then_inc(kept, 1)
                    if k == 10 and norm:
                        inverse_root(mv1[:, :, 1], ve1, rstd1, NT + 1, mv1_done, ve1_done, rstd1_done, c + 2, NT + 1)
                    if k == 14 and norm:
                        q = c + 2
                        pool.wait_ge(xn_done, (NT + 1) * (q + 1))
                        nc.gpsimd.tensor_tensor(h[:, :, :], h[:, :, :], scale_a[:, :, :].broadcast_to([P, NT + 1, D]),
                                                ALU.mult).then_inc(h_scaled, 1)
                        pool.wait_ge(h_scaled, q + 1)
                        nc.gpsimd.tensor_tensor(h[:, :, :], h[:, :, :], shift_a[:, :, :].broadcast_to([P, NT + 1, D]),
                                                ALU.add).then_inc(h_done, 1)
                    if k == 8 and post:
                        q = c - 1
                        inverse_root(mv2[:, :, 1], ve2, rstd2, NT, mv2_done, ve2_done, rstd2_done, q, NT)
                    if k == 9:
                        if post:
                            q = c - 1
                            pool.wait_ge(on_done, NT * (q + 1))
                            nc.gpsimd.tensor_tensor(o[:, :, :], o[:, :, :], gate_g[:, :, :].broadcast_to([P, NT, D]),
                                                    ALU.mult).then_inc(x2_step, 1)
                            pool.wait_ge(x2_step, 3 * q + 1)
                            nc.gpsimd.tensor_tensor(o[:, :, :], o[:, :, :], gate_beta[:, :, :].broadcast_to([P, NT, D]),
                                                    ALU.add).then_inc(x2_step, 1)
                            pool.wait_ge(x2_step, 3 * q + 2)
                            pool.wait_ge(x_res_loaded, MOVES * (q + 1))
                            if later or q >= 1:
                                pool.wait_ge(kept, q)
                                pool.wait_ge(n2_done, NT * q)
                            nc.gpsimd.tensor_tensor(x2[:, :, :], o[:, :, :], x_res[:, :, :], ALU.add).then_inc(x2_step, 1)
                    if k == 1 and prep:
                        q = c + 1
                        pool.wait_ge(work_read, work_count("xc", c))
                        if later or q >= 1:
                            pool.wait_ge(xs_done, q)
                        n = (K + K) * q
                        for tap in range(K):
                            dst = cv if tap == 0 else scratch
                            if tap >= 2:
                                pool.wait_ge(conv_step, n + 2 * tap - 1)
                            if tap == K - 1:
                                pool.wait_ge(work_read, work_count("xc_next", c))
                            nc.gpsimd.tensor_tensor(dst[:, :], xc[:, tap * NB:tap * NB + TOK],
                                                    conv_w_sb[:, tap:tap + 1].broadcast_to([P, TOK]), ALU.mult)\
                              .then_inc(conv_step, 1)
                            if tap >= 1:
                                pool.wait_ge(conv_step, n + 2 * tap)
                                nc.gpsimd.tensor_tensor(cv[:, :], cv[:, :], scratch[:, :], ALU.add).then_inc(conv_step, 1)
                        pool.wait_ge(conv_step, n + 2 * K - 1)
                        nc.gpsimd.tensor_tensor(xc[:, 0:2 * NB], xc[:, TOK:TOK + 2 * NB],
                                                zero_t[:, 0:1].broadcast_to([P, 2 * NB]), ALU.add).then_inc(conv_step, 1)
                    if k == 12 and post:
                        q = c - 1
                        inverse_root(mv3[:, :, 1], ve3, rstd3, NT, mv3_done, ve3_done, rstd3_done, q, NT)
                    if k == 9 and prep:
                        q = c + 1
                        if later or q >= 2:
                            pool.wait_ge(work_read, work_count("proj", c))
                        settle()
                        nc.gpsimd.tensor_tensor(h_res[:, q % 2, :].rearrange("p (j d) -> p j d", j=NT), h[:, 0:NT, :],
                                                out_b_row[:, :, :].broadcast_to([P, NT, D]), ALU.add).then_inc(h_res_done, 1)
                    if k == 13:
                        if post:
                            q = c - 1
                            pool.wait_ge(n2_done, NT * (q + 1))
                            nc.gpsimd.tensor_tensor(h2[:, :, :], h2[:, :, :], scale_b[:, :, :].broadcast_to([P, NT, D]),
                                                    ALU.mult).then_inc(h2_step, 1)
                            pool.wait_ge(h2_step, 2 * q + 1)
                            nc.gpsimd.tensor_tensor(h2[:, :, :], h2[:, :, :], shift_b[:, :, :].broadcast_to([P, NT, D]),
                                                    ALU.add).then_inc(h2_step, 1)
                    if k == 8 and prep:
                        q = c + 1
                        pool.wait_ge(dt_done, q + 1)
                        if later or q >= 1:
                            pool.wait_ge(work_full, work_count("dtx1", c))
                        nc.gpsimd.tensor_tensor(dtx[:, :], dt[:, :], xs[:, :], ALU.mult).then_inc(dtx_done, 1)
                        n = 4 * q
                        part = [dtx_part[:, :, i, :] for i in range(PARTS)]
                        whole, rest = (v[:, :].rearrange("p (t b) -> p t b", b=NB) for v in (dtx, scratch))
                        nought = zero_t[:, 0:1].unsqueeze(2).broadcast_to([P, T, NB])
                        pool.wait_ge(dtx_done, q + 1)
                        nc.gpsimd.tensor_tensor(part[0], whole, nought, ALU.add).then_inc(parts_step, 1)
                        pool.wait_ge(parts_step, n + 1)
                        nc.gpsimd.tensor_tensor(rest, whole, part[0], ALU.subtract).then_inc(parts_step, 1)
                        pool.wait_ge(parts_step, n + 2)
                        nc.gpsimd.tensor_tensor(part[1], rest, nought, ALU.add).then_inc(parts_step, 1)
                        pool.wait_ge(parts_step, n + 3)
                        nc.gpsimd.tensor_tensor(part[2], rest, part[1], ALU.subtract).then_inc(parts_step, 1)
                    for e in range(1, EX):
                        if ffn and read_at(e)[0] == k:
                            q = c - 2
                            pool.wait_ge(work_read, work_count(f"down{e}", c))
                            if e >= 2:
                                pool.wait_ge(acc_step, E * q + e - 1)
                            nc.gpsimd.tensor_tensor(acc[:, :, :], acc[:, :, :],
                                                    scaled[:, e % 2, :].rearrange("p (j d) -> p j d", j=NT),
                                                    ALU.add).then_inc(acc_step, 1)
                    if k == T - 1 and ffn:
                        q = c - 2
                        pool.wait_ge(acc_step, E * (q + 1))
                        nc.gpsimd.tensor_tensor(acc[:, :, :], acc[:, :, :], gate_b[:, :, :].broadcast_to([P, NT, D]),
                                                ALU.mult).then_inc(final_step, 1)
                        pool.wait_ge(final_step, 2 * q + 1)
                        pool.wait_ge(kept, q + 1)
                        nc.gpsimd.tensor_tensor(acc[:, :, :], acc[:, :, :], x2_keep[:, :, :],
                                                ALU.add).then_inc(final_step, 1)

            macros(pool, body)

        @block.scalar
        def _(act):
            for i, (dst, src) in enumerate(params):
                if i % 2 == 1:
                    act.dma_start(dst, src).then_inc(params_in, 16)
            act.wait_ge(params_in, 16 * len(params))
            nc.scalar.activation(cond[:, :], cond[:, :], ACT.Silu).then_inc(cond_ready, 1)
            act.wait_ge(set_up, 2)
            nc.scalar.activation(neg_a[:, :], neg_a[:, :], ACT.Exp).then_inc(a_exp, 1)
            act.wait_ge(started, 1)

            def settle():
                act.wait_ge(started, 1)

            def exp_table():
                act.preload_act_table_set("natural_log_exp_and_others")

            def full(name, c):
                act.wait_ge(work_full, work_count(name, c))

            def decays(half, q, n0, n1):
                if n0 == 0:
                    act.wait_ge(dt_done, q + 1)
                    if not isinstance(q, int) or q >= 1:
                        act.wait_ge(decay_turned, T * (q - 1) + HT * (half + 1))
                for n in range(n0, n1):
                    nc.scalar.activation(decay[:, half * HT:(half + 1) * HT, :, n],
                                         dt[:, half * HT * NB:(half + 1) * HT * NB].rearrange("p (t b) -> p t b", b=NB),
                                         ACT.Exp, scale=neg_a[:, n:n + 1]).then_inc(decay_made[half], 1)

            def gelu(e, q):
                for f in range(FT):
                    act.wait_ge(up_done[f], EX * q + e + 1)
                    if f == 0 and (e >= HBUF or not isinstance(q, int) or q >= 1):
                        old = (e - HBUF, q) if e >= HBUF else (e - HBUF + EX, q - 1)
                        act.wait_ge(work_full, work_count(f"down{old[0]}", old[1] + 2))
                    nc.scalar.activation(hid[:, e % HBUF, f, :], up_ps[f][:, :], ACT.Gelu).then_inc(gelu_done[f], 1)

            def dtx_half(half):
                nc.scalar.activation(dtx_rows[:, half * HT:(half + 1) * HT, :].rearrange("p t d -> p (t d)"),
                                     work[0:PARTS * NB, :].bitcast(BF16), ACT.Copy).then_inc(work_read, 1)

            def scale_inputs(k, q):
                n = T * q + k
                act.wait_ge(input_made, n + 1)
                if not isinstance(q, int) or n >= 2:
                    act.wait_ge(added, n - 1)
                settle()
                for g in range(GV, BG):
                    last = nc.scalar.activation(scaled_in[:, k % 2, g, :], input_ps[:, g, :], ACT.Copy,
                                                scale=b_q[:, q % 2, k * BG + g:k * BG + g + 1])
                last.then_inc(scaled_a, 1)

            def body(c):
                norm, prep, scan, post, ffn = (active(s, c) for s in STAGES)
                later = not isinstance(c, int)
                for k in range(T):
                    if k == 14 and post:
                        full("turn2", c)
                        nc.scalar.activation(h2_t[:, :], work[:, :], ACT.Copy).then_inc(work_read, 1)
                    if k < T - 1 and scan:
                        scale_inputs(k + 1, c)
                    elif k == T - 1 and prep:
                        scale_inputs(0, c + 1)
                    if k == 0 and prep:
                        full("xc", c)
                        if later or c >= 0:
                            act.wait_ge(conv_step, 2 * K * (c + 1))
                        nc.scalar.activation(xc[:, 2 * NB:2 * NB + TOK], work[:, :], ACT.Identity,
                                             bias=in_b_sb[:, 0:1]).then_inc(work_read, 1)
                    if k == 1 and prep:
                        full("turn_next", c)
                        nc.scalar.activation(h_t[:, TOK:], work[:, 0:NB], ACT.Copy).then_inc(work_read, 1)
                    if k == 0 and post:
                        q = c - 1
                        act.wait_ge(y_done, T * (q + 1))
                        if later or q >= 1:
                            act.wait_ge(work_full, work_count("turn_y", c - 1))
                        nc.scalar.activation(y_tok[:, :, :], y_ps[:, :, :], ACT.Copy).then_inc(y_kept, 1)
                    if k == 7 and prep:
                        q = c + 1
                        full("b", c)
                        settle()
                        for i in range(BQ):
                            last = nc.scalar.activation(
                                b_q[i * N:(i + 1) * N, q % 2, :],
                                work[i * N:(i + 1) * N, :].rearrange("p (g b) -> p g b", b=BQ)[:, :, i],
                                ACT.Identity, bias=b_b_col[i * N:(i + 1) * N, 0:1])
                        last.then_inc(work_read, 1)
                    if k == 4 and prep:
                        q = c + 1
                        full("z", c)
                        if later or q >= 2:
                            act.wait_ge(work_read, work_count("turn_y", c))
                        settle()
                        nc.scalar.activation(z_act[:, q % 2, :], work[:, :], ACT.Silu,
                                             bias=in_b_sb[:, 1:2]).then_inc(work_read, 1)
                    if k == 12 and prep:
                        full("dtx0", c)
                        if later or c >= 0:
                            act.wait_ge(input_made, T * c + HT)
                        dtx_half(0)
                    if ffn and k in UP_AT and k in EXP_TABLE_AT:
                        gelu(UP_AT.index(k), c - 2)
                    if k in EXP_TABLE_AT and (prep or k == T - 1 and (norm or post)):
                        exp_table()
                    if k == 15 and norm:
                        full("turn", c)
                        nc.scalar.activation(h_t[:, 0:TOK], work[:, :], ACT.Copy).then_inc(work_read, 1)
                    if k == 1 and ffn:
                        q = c - 2
                        act.wait_ge(gap_done, q + 1)
                        nc.scalar.activation(rt[:, 1, :], rt[:, 0, :], ACT.Exp).then_inc(gap_exp, 1)
                    for at, half, lag, n0, n1 in DECAYS_AT:
                        if at == k and (prep if lag else scan):
                            decays(half, c + lag, n0, n1)
                    if k == 5 and prep:
                        q = c + 1
                        act.wait_ge(work_read, work_count("dt", c))
                        nc.scalar.activation(dt_raw[:, :], dt_raw[:, :], ACT.Exp).then_inc(dt_exp_done, 1)
                        act.wait_ge(dt_exp_done, q + 1)
                        nc.scalar.activation(dt_raw[:, :], dt_raw[:, :], ACT.Ln, bias=1.0).then_inc(dt_log_done, 1)
                    if ffn and k in UP_AT and k not in EXP_TABLE_AT:
                        gelu(UP_AT.index(k), c - 2)
                    if k == 2 and scan:
                        full("dtx1", c)
                        if later or c >= 1:
                            act.wait_ge(input_made, T * c)
                        dtx_half(1)
                    if k == 3 and prep:
                        q = c + 1
                        act.wait_ge(conv_step, 2 * K * q + 2 * K - 1)
                        if later or q >= 1:
                            act.wait_ge(work_full, work_count("c1", c))
                            act.wait_ge(dtx_done, q)
                        nc.scalar.activation(xs[:, :], cv[:, :], ACT.Silu, bias=conv_b_sb[:, 0:1]).then_inc(xs_done, 1)

            macros(act, body)

        @block.vector
        def _(dve):
            nc.vector.memset(x_in[:, NT, :], 0.0).then_inc(set_up, 1)
            dve.wait_ge(params_in, 16 * len(params))
            nc.vector.tensor_scalar(neg_a[:, :], neg_a[:, :], -5.0, 2.0, ALU.max, ALU.min).then_inc(set_up, 1)
            nc.vector.memset(edge[:, 0, :], 1.0).then_inc(set_up, 1)
            nc.vector.memset(group_mask[:, :], 0.0).then_inc(set_up, 1)
            dve.wait_ge(set_up, 4)
            nc.vector.memset(edge[:, 0, CH - 1:CH], 0.0).then_inc(set_up, 1)
            for i in range(BQ):
                nc.vector.memset(group_mask[i * N:(i + 1) * N, i:i + 1], 1.0).then_inc(set_up, 1)
            nc.vector.memset(eps_t[:, :], EPS).then_inc(set_up, 1)
            nc.vector.memset(minus_half[:, :], -0.5).then_inc(set_up, 1)
            nc.vector.memset(zero_t[:, :], 0.0).then_inc(set_up, 1)
            nc.vector.memset(xc[:, 0:2 * NB], 0.0).then_inc(set_up, 1)
            nc.vector.memset(state[:, 1, :], 0.0).then_inc(set_up, 1)
            for e in range(E):
                nc.vector.memset(iota_e[:, 0, e:e + 1], float(e)).then_inc(set_up, 1)
            n = 4 + 1 + BQ + 5 + E
            dve.wait_ge(a_exp, 1)
            nc.vector.tensor_scalar(neg_a[:, :], neg_a[:, :], -1.0, None, ALU.mult).then_inc(set_up, 1)
            n += 1
            dve.wait_ge(mod_ready, 1)
            sa, ca, ga, sb_ = (up_ps[0][:, i * D:(i + 1) * D] for i in range(4))
            cb, gb = (up_ps[1][:, i * D:(i + 1) * D] for i in range(2))
            nc.vector.tensor_copy(shift_a[:, 0, :], sa).then_inc(set_up, 1)
            nc.vector.tensor_scalar(scale_a[:, 0, :], ca, 1.0, None, ALU.add).then_inc(set_up, 1)
            nc.vector.tensor_copy(shift_b[:, 0, :], sb_).then_inc(set_up, 1)
            nc.vector.tensor_scalar(scale_b[:, 0, :], cb, 1.0, None, ALU.add).then_inc(set_up, 1)
            n += 4
            for g, dst in ((ga, gate_t[:, 3, :]), (gb, gate_b[:, 0, :])):
                dve.wait_ge(set_up, n)
                nc.vector.tensor_scalar(gate_t[:, 0, :], g, -1.0, None, ALU.mult).then_inc(set_up, 1)
                nc.vector.tensor_scalar(gate_t[:, 1, :], g, 0.0, 2.0, ALU.is_ge, ALU.mult).then_inc(set_up, 1)
                dve.wait_ge(set_up, n + 2)
                nc.vector.tensor_tensor(gate_t[:, 0, :], g, gate_t[:, 0, :], ALU.max).then_inc(set_up, 1)
                nc.vector.tensor_scalar(gate_t[:, 1, :], gate_t[:, 1, :], -1.0, None, ALU.add).then_inc(set_up, 1)
                dve.wait_ge(set_up, n + 4)
                nc.vector.scalar_tensor_tensor(out=dst, in0=gate_t[:, 0, :], scalar=GATE_MIN, in1=gate_t[:, 1, :],
                                               op0=ALU.max, op1=ALU.mult).then_inc(set_up, 1)
                n += 5
            dve.wait_ge(set_up, n)
            nc.vector.tensor_tensor(gate_g[:, 0, :], gate_t[:, 3, :], g_row[:, :], ALU.mult).then_inc(set_up, 1)
            dve.wait_ge(set_up, n + 1)
            nc.vector.tensor_tensor(gate_beta[:, 0, :], gate_t[:, 3, :], beta_row[:, :], ALU.mult).then_inc(started, 1)

            def settle():
                dve.wait_ge(started, 1)

            def moments(src, bn, mv, tiles, mv_done):
                for j in range(tiles):
                    nc.vector.bn_stats(bn[:, j, :], src[:, j, :])
                nc.vector.drain()
                for j in range(tiles):
                    nc.vector.bn_aggr(mv[:, j, :], bn[:, j, :]).then_inc(mv_done, 1)

            def normalise(dst, src, mv, rstd, tiles, done):
                for j in range(tiles):
                    nc.vector.tensor_scalar(dst[:, j, :], src[:, j, :], mv[:, j, 0:1], rstd[:, j:j + 1],
                                            ALU.subtract, ALU.mult).then_inc(done, 1)

            def full(name, c):
                dve.wait_ge(work_full, work_count(name, c))

            def c_diagonal(half):
                nc.vector.scalar_tensor_tensor(
                    out=c_diag[:, half * HT:(half + 1) * HT, :, 0:BQ].rearrange("p t g b -> p (t g) b"),
                    in0=work[:, 0:TOK // 2].rearrange("p (g b) -> p g b", b=BQ), scalar=c_b_col[:, 0:1],
                    in1=group_mask[:, :].unsqueeze(1).broadcast_to([P, HT * BG, BQ]),
                    op0=ALU.add, op1=ALU.mult).then_inc(work_read, 1)

            def decay_state(k, c):
                n = T * c + k
                dve.wait_ge(input_made, n + 1)
                nc.vector.tensor_tensor(scaled_in[:, k % 2, 0:GV, :], input_ps[:, 0:GV, :],
                                        b_q[:, c % 2, k * BG:k * BG + GV].unsqueeze(2).broadcast_to([P, GV, D]),
                                        ALU.mult).then_inc(scaled_v, 1)
                dve.wait_ge(decay_turned, n + 1)
                if not isinstance(c, int) or n >= 1:
                    dve.wait_ge(state_done, n)
                nc.vector.tensor_tensor(prod[:, :], decay_ps[:, :, :].rearrange("p g d -> p (g d)"),
                                        state[:, (k + 1) % 2, :], ALU.mult).then_inc(decayed, 1)

            def clip_state(k, c):
                n = T * c + k
                dve.wait_ge(scaled_v, n + 1)
                dve.wait_ge(scaled_a, n + 1)
                dve.wait_ge(decayed, n + 1)
                nc.vector.tensor_tensor(prod[:, :], scaled_in[:, k % 2, :, :].rearrange("p g d -> p (g d)"), prod[:, :],
                                        ALU.add).then_inc(added, 1)
                dve.wait_ge(added, n + 1)
                if not isinstance(c, int) or n >= 2:
                    dve.wait_ge(y_done, n - 1)
                nc.vector.tensor_scalar(state[:, k % 2, :], prod[:, :], -CLIP, CLIP, ALU.max,
                                        ALU.min).then_inc(state_done, 1)

            def read_down(e, c):
                q = c - 2
                full(f"down{e}", c)
                if e == 0:
                    if not isinstance(c, int) or q >= 1:
                        dve.wait_ge(stored, MOVES * q)
                    nc.vector.tensor_copy(acc[:, :, :], work[:, :].rearrange("p (j d) -> p j d", d=D))\
                      .then_inc(work_read, 1)
                else:
                    if e >= 3:
                        dve.wait_ge(acc_step, E * q + e - 2)
                    nc.vector.tensor_tensor(
                        scaled[:, e % 2, :].rearrange("p (j d) -> p j d", d=D),
                        work[:, :].rearrange("p (j d) -> p j d", d=D),
                        cw[:, :, e - 1:e].broadcast_to([P, NT, D]), ALU.mult).then_inc(work_read, 1)

            def body(c):
                norm, prep, scan, post, ffn = (active(s, c) for s in STAGES)
                later = not isinstance(c, int)
                for k in range(T):
                    if scan:
                        decay_state(k, c)
                    if k == 4 and scan:
                        full("c1", c)
                        if later or c >= 1:
                            dve.wait_ge(y_done, T * c)
                        c_diagonal(1)
                    if k == 5 and prep:
                        q = c + 1
                        full("dt", c)
                        if later or q >= 1:
                            dve.wait_ge(dt_done, q)
                        nc.vector.tensor_scalar(dt_raw[:, :], work[:, :], dt_b_sb[:, 0:1], DT_IN_MAX, ALU.add,
                                                ALU.min).then_inc(work_read, 1)
                    for e in range(EX):
                        if ffn and read_at(e) == (k, True):
                            read_down(e, c)
                    if scan:
                        clip_state(k, c)
                    if k == 1 and ffn:
                        find_top(c - 2)
                    if k == 4 and ffn:
                        route(c - 2)
                    if k == 2 and prep:
                        q = c + 1
                        full("xc_next", c)
                        if later or q >= 1:
                            dve.wait_ge(conv_step, 2 * K * q)
                        nc.vector.tensor_scalar(xc[:, 2 * NB + TOK:], work[:, 0:NB], in_b_sb[:, 0:1],
                                                edge[:, :, q], ALU.add, ALU.mult).then_inc(work_read, 1)
                    if k == 3 and post:
                        q = c - 1
                        full("turn_y", c)
                        settle()
                        nc.vector.tensor_tensor(yz[:, :], work[:, :], z_act[:, q % 2, :], ALU.mult).then_inc(work_read, 1)
                    if k == 6 and post:
                        q = c - 1
                        full("proj", c)
                        dve.wait_ge(h_res_done, q + 1)
                        if later or q >= 1:
                            dve.wait_ge(x2_step, 3 * q)
                        settle()
                        nc.vector.tensor_tensor(o[:, :, :].rearrange("p j d -> p (j d)"), work[:, :],
                                                h_res[:, q % 2, :], ALU.add).then_inc(work_read, 1)
                    if k == 7 and prep:
                        q = c + 1
                        dve.wait_ge(dt_log_done, q + 1)
                        if later or q >= 1:
                            dve.wait_ge(decay_made[1], N * q)
                            dve.wait_ge(dtx_done, q)
                        nc.vector.tensor_scalar(dt[:, :], dt_raw[:, :], DT_MIN, DT_MAX, ALU.max, ALU.min).then_inc(dt_done, 1)
                    if k == 7 and post:
                        dve.wait_ge(work_read, work_count("proj", c))
                        moments(o, bn2, mv2, NT, mv2_done)
                    if k == 8 and post:
                        q = c - 1
                        dve.wait_ge(rstd2_done, q + 1)
                        normalise(o, o, mv2, rstd2, NT, on_done)
                    if k == 11 and prep:
                        full("c0", c)
                        if later or c >= 0:
                            dve.wait_ge(y_done, T * c + HT)
                        else:
                            dve.wait_ge(diag_clear, 1)
                        c_diagonal(0)
                    if k == 11 and post:
                        q = c - 1
                        dve.wait_ge(x2_step, 3 * (q + 1))
                        moments(x2, bn3, mv3, NT, mv3_done)
                    if k == 12 and post:
                        q = c - 1
                        dve.wait_ge(rstd3_done, q + 1)
                        if later or q >= 1:
                            dve.wait_ge(work_full, work_count("turn2", c - 1))
                        normalise(h2, x2, mv3, rstd3, NT, n2_done)
                    if k == 9 and norm:
                        dve.wait_ge(x_loaded, LOADS * (c + 3))
                        moments(x_in, bn1, mv1, NT + 1, mv1_done)
                    if k == 15 and post:
                        full("logits", c)
                        nc.vector.tensor_copy(lg[:, :, :], work[:, 0:NT * E].rearrange("p (j e) -> p j e", e=E))\
                          .then_inc(work_read, 1)
                    if k == 10 and not later and c == -2:
                        nc.vector.memset(c_diag[:, :, :, :], 0.0).then_inc(diag_clear, 1)
                    if k == 13 and norm:
                        q = c + 2
                        dve.wait_ge(rstd1_done, q + 1)
                        if later or q >= 1:
                            dve.wait_ge(work_full, work_count("turn_next", c))
                            dve.wait_ge(h_res_done, q)
                        normalise(h, x_in, mv1, rstd1, NT + 1, xn_done)
                    for e in range(EX):
                        if ffn and read_at(e) == (k, False):
                            read_down(e, c)

            def find_top(q):
                nc.vector.drain()
                for j in range(NT):
                    nc.vector.max(top_v[:, j, :], lg[:, j, :])
                nc.vector.drain()
                nc.vector.tensor_tensor(rt[:, 0, :], top_v[:, :, 1], top_v[:, :, 0], ALU.subtract).then_inc(gap_done, 1)
                for j in range(NT):
                    nc.vector.max_index(top_i[:, j, :], top_v[:, j, :], lg[:, j, :]).then_inc(index_done, 1)

            def route(q):
                dve.wait_ge(index_done, NT * (q + 1))
                nc.vector.tensor_copy(top_f[:, :, :], top_i[:, :, 0:2]).then_inc(route_step, 1)
                dve.wait_ge(gap_exp, q + 1)
                n = 9 * q
                nc.vector.tensor_scalar(rt[:, 2, :], rt[:, 1, :], 1.0, None, ALU.add).then_inc(route_step, 1)
                dve.wait_ge(route_step, n + 2)
                nc.vector.reciprocal(rt[:, 3, :], rt[:, 2, :]).then_inc(route_step, 1)
                dve.wait_ge(route_step, n + 3)
                nc.vector.tensor_tensor(rt[:, 2, :], rt[:, 1, :], rt[:, 3, :], ALU.mult).then_inc(route_step, 1)
                for i in range(2):
                    nc.vector.tensor_tensor(pick[:, i, :, :], iota_e[:, :, :].broadcast_to([P, NT, E]),
                                            top_f[:, :, i:i + 1].broadcast_to([P, NT, E]), ALU.is_equal).then_inc(route_step, 1)
                dve.wait_ge(route_step, n + 6)
                for i, share in enumerate((3, 2)):
                    nc.vector.tensor_tensor(pick[:, i, :, :], pick[:, i, :, :],
                                            rt[:, share, :].unsqueeze(2).broadcast_to([P, NT, E]), ALU.mult).then_inc(route_step, 1)
                dve.wait_ge(route_step, n + 8)
                nc.vector.tensor_tensor(cw[:, :, :], pick[:, 0, :, :], pick[:, 1, :, :], ALU.add).then_inc(route_step, 1)

            macros(dve, body)

        @block.tensor
        def _(pe):
            pe.wait_ge(cond_ready, 1)
            nc.tensor.matmul(up_ps[0][:, :], cond[:, :], wmod_sb[:, 0:4 * D], start=True, stop=True)
            nc.tensor.matmul(up_ps[1][:, 0:2 * D], cond[:, :], wmod_sb[:, 4 * D:], start=True, stop=True).then_inc(mod_ready, 1)
            pe.wait_ge(started, 1)
            pe.wait_ge(diag_set, 1)
            pe.wait_ge(ident_set, 3)

            def free_work(name, c):
                count = work_count(name, c) - 1
                if not isinstance(c, int) or count >= 1:
                    pe.wait_ge(work_read, count)

            def turn_decays(k, q):
                n = T * q + k
                if k % HT == 0:
                    pe.wait_ge(decay_made[k // HT], N * (q + 1))
                if not isinstance(q, int) or n >= 1:
                    pe.wait_ge(decayed, n)
                for g in range(BG):
                    last = nc.tensor.transpose(decay_ps[:, g, :],
                                               decay[:, k, g * BQ:(g + 1) * BQ, :].rearrange("p b n -> p (b n)"), ident[:, :])
                last.then_inc(decay_turned, 1)

            def make_inputs(k, q):
                n = T * q + k
                if k == 0:
                    pe.wait_ge(work_read, work_count("dtx0", q - 1))
                if k == HT:
                    pe.wait_ge(work_read, work_count("dtx1", q))
                if not isinstance(q, int) or n >= 1:
                    pe.wait_ge(scaled_v, n)
                    pe.wait_ge(scaled_a, n)
                for g in range(BG):
                    last = nc.tensor.matmul(input_ps[:, g, :],
                                            spread[:, g * BQ:(g + 1) * BQ, :].rearrange("p b n -> p (b n)"),
                                            dtx_rows[:, k, :], start=True, stop=True)
                last.then_inc(input_made, 1)

            def read_out(k, q):
                n = T * q + k
                pe.wait_ge(state_done, n + 1)
                if k == 0:
                    pe.wait_ge(work_read, work_count("c0", q - 1))
                    if not isinstance(q, int) or q >= 1:
                        pe.wait_ge(y_kept, q)
                if k == HT:
                    pe.wait_ge(work_read, work_count("c1", q))
                blocks = c_diag[:, k, :, :].rearrange("p g b -> p (g b)")
                for g in range(BG):
                    last = nc.tensor.matmul(y_ps[rows(k % SPT), k // SPT, :], blocks[:, g * NB:(g + 1) * NB],
                                            state[:, k % 2, g * D:(g + 1) * D], start=(g == 0), stop=(g == BG - 1))
                last.then_inc(y_done, 1)

            def turn(src, tiles):
                for i, j in enumerate(tiles):
                    last = nc.tensor.transpose(work[:, i * P:(i + 1) * P], src(j), ident[:, :])
                return last

            def use(name, c):
                free_work(name, c)
                if name in ("dtx0", "dtx1"):
                    q = c + 1 if name == "dtx0" else c
                    pe.wait_ge(parts_step, 4 * (q + 1))
                    pe.wait_ge(diag_set, PARTS + 1)
                    for t in range(HT):
                        last = nc.tensor.transpose(
                            work[0:PARTS * NB, :].bitcast(BF16)[:, t * D:(t + 1) * D],
                            dtx_part[:, int(name[-1]) * HT + t, :, :].rearrange("p i b -> p (i b)"), ident_b[:, :])
                elif name in ("c0", "c1"):
                    q = c + 1 if name == "c0" else c
                    pe.wait_ge(xs_done, q + 1)
                    half = int(name[-1]) * TOK // 2
                    last = nc.tensor.matmul(work[:, 0:TOK // 2], c_w_sb[:, :], xs[:, half:half + TOK // 2], start=True, stop=True)
                elif name == "turn":
                    pe.wait_ge(h_done, c + 3)
                    last = turn(lambda j: h[:, j, :], range(NT))
                elif name == "turn_next":
                    last = turn(lambda j: h[:, j, :], [NT])
                elif name == "xc":
                    last = nc.tensor.matmul(work[:, :], in_w_sb[:, 0:D], h_t[:, 0:TOK], start=True, stop=True)
                elif name == "xc_next":
                    last = nc.tensor.matmul(work[:, 0:NB], in_w_sb[:, 0:D], h_t[:, TOK:], start=True, stop=True)
                elif name == "z":
                    last = nc.tensor.matmul(work[:, :], in_w_sb[:, D:], h_t[:, 0:TOK], start=True, stop=True)
                elif name == "dt":
                    pe.wait_ge(xs_done, c + 2)
                    last = nc.tensor.matmul(work[:, :], dt_w_sb[:, :], xs[:, :], start=True, stop=True)
                elif name == "b":
                    last = nc.tensor.matmul(work[:, :], b_w_sb[:, :], xs[:, :], start=True, stop=True)
                elif name == "turn_y":
                    pe.wait_ge(y_kept, c)
                    last = turn(lambda j: y_tok[:, j, :], range(NT))
                elif name == "proj":
                    for j in range(NT):
                        last = nc.tensor.matmul(work[:, j * D:(j + 1) * D], yz[:, j * P:(j + 1) * P], out_w_sb[:, :],
                                                start=True, stop=True)
                elif name == "turn2":
                    pe.wait_ge(h2_step, 2 * c)
                    last = turn(lambda j: h2[:, j, :], range(NT))
                elif name == "logits":
                    for j in range(NT):
                        last = nc.tensor.matmul(work[:, j * E:(j + 1) * E], h2_t[:, j * P:(j + 1) * P], wg_sb[:, :],
                                                start=True, stop=True)
                else:
                    e = int(name[4:])
                    for f in range(FT):
                        pe.wait_ge(gelu_done[f], EX * (c - 2) + e + 1)
                    for j in range(NT):
                        for f in range(FT):
                            last = nc.tensor.matmul(work[:, j * D:(j + 1) * D], hid[:, e % HBUF, f, j * P:(j + 1) * P],
                                                    wd_sb[:, e, f, :], start=(f == 0), stop=(f == FT - 1))
                last.then_inc(work_full, 1)

            def uses(k, place, c):
                for where, stage, name in at_step(k):
                    if where == place and active(stage, c):
                        use(name, c)

            def up(e, q):
                for f in range(FT):
                    if e >= 1 or not isinstance(q, int) or q >= 1:
                        pe.wait_ge(gelu_done[f], EX * q + e)
                    nc.tensor.matmul(up_ps[f][:, :], wu_sb[:, e, f * P:(f + 1) * P], h2_t[:, :], start=True, stop=True)\
                      .then_inc(up_done[f], 1)

            def body(c):
                norm, prep, scan, post, ffn = (active(s, c) for s in STAGES)
                for k in range(T):
                    if k < T - 1 and scan:
                        turn_decays(k + 1, c)
                        make_inputs(k + 1, c)
                    elif k == T - 1 and prep:
                        turn_decays(0, c + 1)
                        make_inputs(0, c + 1)
                    if k == 0 and post:
                        read_out(T - 1, c - 1)
                    elif k > 0 and scan:
                        read_out(k - 1, c)
                    uses(k, "a", c)
                    if ffn:
                        if k == 0:
                            if isinstance(c, int) and c == 2:
                                pe.wait_ge(ffn_in, 32)
                            pe.wait_ge(work_read, work_count("turn2", c - 1))
                        for e in range(EX):
                            if UP_AT[e] == k:
                                up(e, c - 2)
                    uses(k, "b", c)

            macros(pe, body)


_INS = ["x", "in_w", "in_b", "conv_w", "conv_b", "a_log", "b_w", "b_b", "c_w", "c_b", "dt_w", "dt_b", "out_w",
        "out_b", "ln_g", "ln_beta", "wg", "wu", "wd", "c_t", "wmod"]


def kernel(**inputs):
    import concourse.bacc as _bacc
    from concourse.bass_utils import run_bass_kernel_spmd as _run

    g = {name[3:]: np.asarray(a) for name, a in inputs.items()}

    def rows_of(v):
        return np.broadcast_to(v, (P, v.shape[0]))

    laid = {
        "x": g["attn_x"],
        "in_w": g["attn_in_proj_w"].T,
        "in_b": g["attn_in_proj_b"].reshape(2, D).T,
        "conv_w": g["attn_conv_w"].reshape(D, K),
        "conv_b": g["attn_conv_b"].reshape(D, 1),
        "a_log": g["attn_A_log"],
        "b_w": np.tile(g["attn_B_w"].T, (1, BQ)),
        "b_b": np.tile(g["attn_B_b"], BQ).reshape(P, 1),
        "c_w": np.tile(g["attn_C_w"].T, (1, BQ)),
        "c_b": np.tile(g["attn_C_b"], BQ).reshape(P, 1),
        "dt_w": g["attn_dt_w"].T,
        "dt_b": g["attn_dt_b"].reshape(D, 1),
        "out_w": g["attn_out_w"].T,
        "out_b": rows_of(g["attn_out_b"]),
        "ln_g": rows_of(g["attn_ln_g"]),
        "ln_beta": rows_of(g["attn_ln_beta"]),
        "wg": g["ffn_Wg"],
        "wu": np.concatenate([g["ffn_W1"][None], g["ffn_Wu"]]).transpose(1, 0, 2),
        "wd": np.concatenate([g["ffn_W2"][None], g["ffn_Wd"]]).reshape(EX, FT, P, D).transpose(2, 0, 1, 3),
        "c_t": np.tile(g["c"].T, (1, SPT)),
        "wmod": g["wmod"],
    }
    nc = _bacc.Bacc("TRN2", target_bir_lowering=False, num_devices=1)
    arrays, args = {}, []
    for name in _INS:
        a = np.ascontiguousarray(laid[name])
        arrays[f"in_{name}"] = a
        args.append(nc.dram_tensor(f"in_{name}", a.shape, mybir.dt.from_np(a.dtype), kind="ExternalInput").ap())
    args.append(nc.dram_tensor("out_y", (NB, L, D), F32, kind="ExternalOutput").ap())
    adaln_block(nc, *args)
    r = _run(nc, [arrays], core_ids=[0])
    return r.results[0]["out_y"]
```
